# Optimizing a Trainium2 kernel written in Bass

```python
import numpy as np
import jax
import jax.numpy as jnp

def _softmax(x, axis=-1):
    return jax.nn.softmax(x, axis=axis)

def _gelu(x):
    return jax.nn.gelu(x, approximate=True)

def _silu(x):
    return jax.nn.silu(x)

def _sigmoid(x):
    return jax.nn.sigmoid(x)

def _layernorm(x, axis=-1, eps=1e-05):
    m = jnp.mean(x, axis=axis, keepdims=True)
    v = jnp.var(x, axis=axis, keepdims=True)
    return (x - m) / jnp.sqrt(v + eps)

def _scatter_add(tgt, idx, src, axis=0):
    return tgt.at[idx].add(src)

def _segment_sum(src, seg, n):
    return jax.ops.segment_sum(src, seg, n)
kernel_name = 'mk_prb_d1_jaxref_r8_53a8ca'

def setup_inputs(seed: int=0):
    np.random.seed(seed)
    _w = jnp.asarray

    def _L0_attn_setup():
        import math
        import jax, jax.numpy as jnp
        import numpy as np
        B, T, C, H = (1, 512, 128, 16)
        HD = C // H

        def get_slopes(n):

            def pow2(n):
                start = 2 ** (-2 ** (-(math.log2(n) - 3)))
                return [start * start ** i for i in range(n)]
            if math.log2(n).is_integer():
                return pow2(n)
            cp2 = 2 ** math.floor(math.log2(n))
            return pow2(cp2) + get_slopes(2 * cp2)[0::2][:n - cp2]
        key = jax.random.key(seed)
        ks = jax.random.split(key, 5)
        x = jax.random.normal(ks[0], (B, T, C), dtype=jnp.float32)
        mk = lambda k: 0.02 * jax.random.normal(k, (C, C), dtype=jnp.float32)
        return {'x': x, 'Wq': mk(ks[1]), 'bq': jnp.zeros((C,), jnp.float32), 'Wk': mk(ks[2]), 'bk': jnp.zeros((C,), jnp.float32), 'Wv': mk(ks[3]), 'bv': jnp.zeros((C,), jnp.float32), 'Wo': 0.02 / math.sqrt(24) * jax.random.normal(ks[4], (C, C), dtype=jnp.float32), 'bo': jnp.zeros((C,), jnp.float32)}
    _L0_attn_in = _L0_attn_setup()

    def _L0_ffn_setup():
        import jax, jax.numpy as jnp
        import numpy as np
        D_MODEL = 128
        HIDDEN = 512
        NUM_EXPERTS = 8
        TOP_K = 2
        DEPTH = 12
        DEPTH_SCALE = 1.0 / np.sqrt(DEPTH)
        key = jax.random.key(seed)
        k_x, k_r, k_g, k_u, k_d = jax.random.split(key, 5)
        s_in = 1.0 / np.sqrt(D_MODEL)
        s_hid = 1.0 / np.sqrt(HIDDEN)
        return {'x': jax.random.normal(k_x, (2, 256, D_MODEL), dtype=jnp.float32), 'Wr': jax.random.normal(k_r, (D_MODEL, NUM_EXPERTS), dtype=jnp.float32) * s_in, 'Wg': jax.random.normal(k_g, (NUM_EXPERTS, D_MODEL, HIDDEN), dtype=jnp.float32) * s_in, 'Wu': jax.random.normal(k_u, (NUM_EXPERTS, D_MODEL, HIDDEN), dtype=jnp.float32) * s_in, 'Wd': jax.random.normal(k_d, (NUM_EXPERTS, HIDDEN, D_MODEL), dtype=jnp.float32) * s_hid}
    _L0_ffn_in = _L0_ffn_setup()
    _d = {'L0_attn_x': _L0_attn_in['x'], 'L0_attn_Wq': _L0_attn_in['Wq'], 'L0_attn_bq': _L0_attn_in['bq'], 'L0_attn_Wk': _L0_attn_in['Wk'], 'L0_attn_bk': _L0_attn_in['bk'], 'L0_attn_Wv': _L0_attn_in['Wv'], 'L0_attn_bv': _L0_attn_in['bv'], 'L0_attn_Wo': _L0_attn_in['Wo'], 'L0_attn_bo': _L0_attn_in['bo'], 'L0_ffn_Wr': _L0_ffn_in['Wr'], 'L0_ffn_Wg': _L0_ffn_in['Wg'], 'L0_ffn_Wu': _L0_ffn_in['Wu'], 'L0_ffn_Wd': _L0_ffn_in['Wd']}
    _x0 = _d['L0_attn_x']
    _d['L0_attn_x'] = jax.random.normal(jax.random.fold_in(jax.random.key(seed), 1), (4, 1024, 128), dtype=_x0.dtype)
    del _x0
    return _d

def reference(L0_attn_x, L0_attn_Wq, L0_attn_bq, L0_attn_Wk, L0_attn_bk, L0_attn_Wv, L0_attn_bv, L0_attn_Wo, L0_attn_bo, L0_ffn_Wr, L0_ffn_Wg, L0_ffn_Wu, L0_ffn_Wd):

    def _L0_attn_ref(x, Wq, bq, Wk, bk, Wv, bv, Wo, bo):
        import math
        import jax, jax.numpy as jnp
        import numpy as np
        B, T, C, H = (1, 512, 128, 16)
        HD = C // H

        def get_slopes(n):

            def pow2(n):
                start = 2 ** (-2 ** (-(math.log2(n) - 3)))
                return [start * start ** i for i in range(n)]
            if math.log2(n).is_integer():
                return pow2(n)
            cp2 = 2 ** math.floor(math.log2(n))
            return pow2(cp2) + get_slopes(2 * cp2)[0::2][:n - cp2]
        b, t, c = x.shape
        proj = lambda W, bias: (x @ W + bias).reshape(b, t, H, HD).transpose(0, 2, 1, 3)
        q, k, v = (proj(Wq, bq), proj(Wk, bk), proj(Wv, bv))
        scale = 1.0 / jnp.sqrt(jnp.asarray(HD, x.dtype))
        attn = jnp.einsum('bhqd,bhkd->bhqk', q, k) * scale
        slopes = jnp.asarray(get_slopes(H), dtype=x.dtype)
        alibi = -slopes[:, None, None] * (t - 1 - jnp.arange(t, dtype=x.dtype))[None, None, :]
        attn = attn + alibi
        causal = jnp.tril(jnp.ones((t, t), dtype=bool))[None, None]
        attn = jnp.where(causal, attn, jnp.finfo(x.dtype).min)
        p = jax.nn.softmax(attn, axis=-1)
        out = jnp.einsum('bhqk,bhkd->bhqd', p, v).transpose(0, 2, 1, 3).reshape(b, t, c)
        return out @ Wo + bo

    def _L0_ffn_ref(x, Wr, Wg, Wu, Wd):
        import jax, jax.numpy as jnp
        import numpy as np
        D_MODEL = 128
        HIDDEN = 512
        NUM_EXPERTS = 8
        TOP_K = 2
        DEPTH = 12
        DEPTH_SCALE = 1.0 / np.sqrt(DEPTH)
        B, T, C = x.shape
        flat_x = x.reshape(-1, C)
        logits = flat_x @ Wr
        top_vals, top_idx = jax.lax.top_k(logits, TOP_K)
        rw = jax.nn.softmax(top_vals.astype(jnp.float32), axis=-1).astype(x.dtype)
        combine = jnp.sum(rw[..., None] * jax.nn.one_hot(top_idx, NUM_EXPERTS, dtype=x.dtype), axis=1)
        g = jnp.einsum('nc,ech->neh', flat_x, Wg)
        u = jnp.einsum('nc,ech->neh', flat_x, Wu)
        h = jax.nn.silu(g) * u
        eo = jnp.einsum('neh,ehc->nec', h, Wd) * DEPTH_SCALE
        out = jnp.einsum('ne,nec->nc', combine, eo)
        return out.reshape(B, T, C)
    x = L0_attn_x
    xn = _layernorm(x, axis=-1)
    x = x + _L0_attn_ref(xn, L0_attn_Wq, L0_attn_bq, L0_attn_Wk, L0_attn_bk, L0_attn_Wv, L0_attn_bv, L0_attn_Wo, L0_attn_bo) + _L0_ffn_ref(xn, L0_ffn_Wr, L0_ffn_Wg, L0_ffn_Wu, L0_ffn_Wd)
    return x

_drawn_inputs = setup_inputs


def setup_inputs(seed=0):
    import zlib

    import numpy as np

    out = dict(_drawn_inputs(seed))
    spreads = {'L0_attn_bq': (0.0, 0.8),
     'L0_attn_bk': (0.0, 0.8),
     'L0_attn_bv': (0.0, 0.8),
     'L0_attn_bo': (0.0, 0.1)}
    factors = {'L0_attn_Wq': 8.0, 'L0_attn_Wk': 8.0, 'L0_attn_Wv': 8.0, 'L0_attn_Wo': 8.0}
    for name, (base, spread) in spreads.items():
        noise = np.random.default_rng([zlib.crc32(name.encode()), seed]).standard_normal(out[name].shape)
        drawn = base * np.exp(spread * noise) if base else spread * noise
        out[name] = jnp.asarray(drawn.astype(out[name].dtype))
    for name, factor in factors.items():
        out[name] = (out[name] * factor).astype(out[name].dtype)
    return out
```

```python
import numpy as np
import concourse.bass as bass
from concourse import mybir
from contextlib import ExitStack

fp32 = mybir.dt.float32
bf16 = mybir.dt.bfloat16
i32 = mybir.dt.int32
u32 = mybir.dt.uint32
u16 = mybir.dt.uint16
ALU = mybir.AluOpType
ACT = mybir.ActivationFunctionType
AX = mybir.AxisListType

P = 128
B, T, C = 4, 1024, 128
H, HD = 16, 8
N = B * T
NT = N // P
BT = T // P
HG = 4
NHG = H // HG
G = B * NHG
HALF = T // 2
QT = HALF // P
PARTS = 3
SPLIT = PARTS * PARTS * HD
ROW_ONE = SPLIT
ROW_MAX = SPLIT + PARTS
ROWS = SPLIT + 2 * PARTS
STEP = 4
STEPS = P // STEP - 1
ROWS_DIAG = ROWS + STEPS
E, TOPK, HID = 8, 2, 512
HC = HID // P
SLOT_TILES = N * TOPK // P + E
ROW = C + 2
PAD = 8
NEG = -3.0e38
EPS = 1e-5
DEPTH_SCALE = 1.0 / np.sqrt(12)

UNITS = 12
SEQ0 = UNITS * HG + 1
SEQ = UNITS * HG + 2


class Count:

    def __init__(self, c, i=None, a=0):
        self.c, self.i, self.a = c, i, a

    def __add__(self, k):
        return Count(self.c + k, self.i, self.a)

    def __mul__(self, k):
        return Count(self.c * k, self.i, self.a * k)

    def __floordiv__(self, k):
        assert self.a % k == 0
        return Count(self.c // k, self.i, self.a // k)

    def __mod__(self, k):
        assert self.a % k == 0
        return self.c % k

    def v(self):
        return self.c if self.i is None else self.i * self.a + self.c


def max_unit(u):
    if u < 4:
        return u, 0, P * (u + 1), True
    if u < 8:
        return u, 0, HALF, False
    return u - 4, 1, P * (u - 7), True


def prob_unit(u):
    if u < 4:
        return 0, u, P * u, True
    if u < 8:
        return 1, u - 4, 0, False
    return 1, u - 4, P * (u - 8), True


def truncated_parts(a):
    parts, rest = [], a.astype(np.float32)
    for _ in range(PARTS):
        bits = rest.view(np.uint32) & np.uint32(0xFFFF0000)
        parts.append((bits >> 16).astype(np.uint16))
        rest = rest - bits.view(np.float32)
    return parts


def constants(nc):
    start = 2.0 ** (-2.0 ** -(np.log2(H) - 3))
    slopes = np.array([start * start ** i for i in range(H)], np.float32)
    bias = -slopes[:, None] * (T - 1 - np.arange(T, dtype=np.float32))[None, :]
    parts = np.stack(truncated_parts(bias), 1)
    parts = parts.reshape(NHG, HG, PARTS, T).transpose(0, 2, 1, 3)
    alibi = np.tile(parts, (B, 1, 1, 1))
    i = np.arange(P)
    causal = np.zeros((P, HALF), np.float32)
    causal[:, HALF - P:] = np.where(i[None, :] <= i[:, None], 0.0, NEG)
    edge = STEP * (1 + np.arange(STEPS))[:, None]
    stairs_q = np.where(i[None, :] < edge, 0x3F80, 0).astype(np.uint16)
    stairs_k = np.where(i[None, :] >= edge, 0xF149, 0).astype(np.uint16)
    before = np.where(i[:, None] < i[None, :], 0x3F80, 0).astype(np.uint16)
    return (nc.inline_tensor(np.ascontiguousarray(alibi), name="alibi_parts"),
            nc.inline_tensor(np.eye(P, dtype=np.float32), name="identity"),
            nc.inline_tensor(causal, name="causal_bias"),
            nc.inline_tensor(before, name="before_in_tile"),
            nc.inline_tensor(stairs_q, name="stairs_q"), nc.inline_tensor(stairs_k, name="stairs_k"))


def build(nc, x, Wq, bq, Wk, bk, Wv, bv, Wo, bo, Wr, Wg, Wu, Wd, out):
    alibi, eye, causal, before, stairs_q, stairs_k = [t.ap() for t in constants(nc)]
    q_split = nc.dram_tensor("q_split", [G, HG, (2 * PARTS - 1) * HD, T], bf16).ap()
    k_split = nc.dram_tensor("k_split", [G, HG, PARTS * HD, T], bf16).ap()
    slots = nc.dram_tensor("slots", [SLOT_TILES * P, ROW], fp32).ap()
    routed = nc.dram_tensor("routed", [N * TOPK + PAD * P, C], fp32).ap()

    ctx = ExitStack()
    with ctx:
        def sb(name, shape, dt=fp32):
            return ctx.enter_context(nc.sbuf_tensor(name, shape, dt))

        def sem(name):
            return ctx.enter_context(nc.semaphore(name))

        def sems(name, n=2):
            return [sem(f"{name}{i}") for i in range(n)]

        ps = ctx.enter_context(nc.psum_tensor("ps", [P, 8, HALF], fp32))

        xn = sb("xn", [P, NT * C])
        vall = sb("vall", [P, G * BT * HG * HD])
        attn = sb("attn", [P, G * BT * HG * HD])
        weights = sb("weights", [P, E * 3 * HID])
        wg_sb = weights[:, 0:E * HID]
        wu_sb = weights[:, E * HID:2 * E * HID]
        wd_sb = weights[:, 2 * E * HID:3 * E * HID]
        xb = [weights[:, 0:T], weights[:, T:2 * T]]
        sq = weights[:, 2 * T:3 * T]
        xt = [weights[:, 3 * T:4 * T], weights[:, 4 * T:5 * T]]
        full = [weights[:, 5 * T:6 * T], weights[:, 6 * T:7 * T]]
        rest = [weights[:, 7 * T:8 * T], weights[:, 8 * T:9 * T]]
        prob_sb = sb("prob_sb", [P, 2 * HG * HALF])
        prob = [prob_sb[:, i * HG * HALF:(i + 1) * HG * HALF].rearrange("p (c t) -> p c t", c=HG) for i in range(2)]
        split = [a.bitcast(bf16).rearrange("p (s i t) -> p s i t", s=2, i=PARTS)
                 for a in (weights[:, 9 * T:12 * T], prob_sb[:, 0:3 * T])]
        qs = [sb(f"qs{i}", [ROWS_DIAG, 2, HG, HALF], bf16) for i in range(2)]
        ks = [sb(f"ks{i}", [ROWS_DIAG, 2, HG, HALF], bf16) for i in range(2)]
        vs = [sb(f"vs{i}", [P, BT, HG, 32]) for i in range(2)]
        ot = [sb(f"ot{i}", [P, HALF]) for i in range(2)]
        causal_sb = sb("causal_sb", [P, HALF])
        junk = [sb(f"junk{i}", [P, HALF], bf16) for i in range(2)]
        ident = sb("ident", [P, P])
        before_sb = sb("before_sb", [P, P], bf16)
        ones_bf = sb("ones_bf", [P, P], bf16)
        wq_sb, wk_sb, wv_sb, wo_sb = [sb(n, [P, C]) for n in ("wq_sb", "wk_sb", "wv_sb", "wo_sb")]
        wr_sb = sb("wr_sb", [P, E])
        bias_qk = sb("bias_qk", [P, 2])
        bias_q_scaled = sb("bias_q_scaled", [P, 1])
        bv_row = sb("bv_row", [P, C])
        bo_row = sb("bo_row", [P, C])
        stat = sb("stat", [P, 5, BT])
        mx = sb("mx", [P, 2, HG * QT])
        mx_late = sb("mx_late", [P, HG * QT])
        mx_all = sb("mx_all", [P, HG * QT])
        mt = [sb(f"mt{i}", [HG * QT, PARTS, P], bf16) for i in range(2)]
        mrest = sb("mrest", [HG * QT, P])
        rden = sb("rden", [P, 2, HG * QT])
        logits = sb("logits", [P, NT * E])
        rt = [sb(f"rt{i}", [P, NT * E]) for i in range(6)]
        mask_bf = sb("mask_bf", [P, NT * E], bf16)
        rs = sb("rs", [P, 5, NT])
        ex = sb("ex", [P, 6, E])
        exi = sb("exi", [P, 2, E], i32)
        eidx = sb("eidx", [P, NT * E])
        meta = sb("meta", [P, NT, TOPK, 3])
        tile_no = sb("tile_no", [1, SLOT_TILES])
        owner = sb("owner", [1, SLOT_TILES * E])
        owner_f = sb("owner_f", [1, SLOT_TILES])
        owner_i = sb("owner_i", [1, SLOT_TILES], i32)
        stage = [sb(f"stage{i}", [P, ROW]) for i in range(2)]
        stage_idx = [sb(f"stage_idx{i}", [P, 1], u32) for i in range(2)]
        padrow = sb("padrow", [P, PAD, ROW])
        row_in = [sb(f"row_in{i}", [P, ROW]) for i in range(4)]
        row_t = [sb(f"row_t{i}", [P, P]) for i in range(2)]
        gate = [sb(f"gate{i}", [P, HID]) for i in range(2)]
        hid = [sb(f"hid{i}", [P, HID]) for i in range(2)]
        hid_t = [sb(f"hid_t{i}", [P, HID]) for i in range(2)]
        y_out = [sb(f"y_out{i}", [P, C]) for i in range(2)]
        y_idx = [sb(f"y_idx{i}", [P, 1], u32) for i in range(4)]
        heads = ot
        at_sb = hid
        xres = gate
        xbo = hid_t
        yres = [prob_sb[:, i * 2 * HALF:(i + 1) * 2 * HALF] for i in range(2)]
        fin = [prob_sb[:, (4 + i) * HALF:(5 + i) * HALF] for i in range(2)]

        s_const, s_bias, s_stairs, s_ones, s_stack_ones, s_pad, s_padded, s_iota = [sem("s_" + n) for n in (
            "const", "bias", "stairs", "ones", "stack_ones", "pad", "padded", "iota")]
        s_x, s_rest, s_part2, s_part3, s_split = [sems("s_" + n) for n in ("x", "rest", "part2", "part3", "split")]
        s_xc, s_sq, s_var, s_std, s_ln, s_xn, s_xt_ps, s_xt, s_qk_ps, s_qk, s_v_ps, s_v, s_lg_ps, s_lg = [
            sem("s_" + n) for n in ("xc", "sq", "var", "std", "ln", "xn", "xt_ps", "xt", "qk_ps", "qk", "v_ps", "v",
                                    "lg_ps", "lg")]
        s_rt, s_gap, s_gap_exp, s_mask, s_count, s_meta, s_owner, s_weights = [sem("s_" + n) for n in (
            "rt", "gap", "gap_exp", "mask", "count", "meta", "owner", "weights")]
        s_load = [sems(f"s_load{i}_") for i in range(2)]
        s_chunk = sem("s_chunk")
        s_read = sem("s_read")
        s_mx = sem("s_mx")
        s_mpart = sem("s_mpart")
        s_mt = sem("s_mt")
        s_mrow = sems("s_mrow")
        s_score = sem("s_score")
        s_exp = sem("s_exp")
        s_causal = sem("s_causal")
        s_vcopy = sem("s_vcopy")
        s_pv = sem("s_pv")
        s_ocopy = sem("s_ocopy")
        s_ot = sem("s_ot")
        s_rden = sem("s_rden")
        s_norm = sem("s_norm")
        s_staged = sem("s_staged")
        s_scatter = sems("s_scatter")
        s_heads, s_at_ps, s_at, s_wo, s_xbo, s_res = [sem("s_" + n) for n in ("heads", "at_ps", "at", "wo", "xbo", "res")]
        s_xres = sems("s_xres")
        s_row = sems("s_row", 4)
        s_row_ps, s_row_t, s_gate_ps, s_up_ps, s_gate, s_hid, s_hid_ps, s_hid_t, s_y_ps, s_y, s_yidx = [
            sem("s_" + n) for n in ("row_ps", "row_t", "gate_ps", "up_ps", "gate", "hid", "hid_ps", "hid_t", "y_ps",
                                    "y", "yidx")]
        s_routed = sems("s_routed")
        s_yres = sems("s_yres")
        s_acc, s_fin = sem("s_acc"), sem("s_fin")
        s_out = sems("s_out")

        block = ctx.enter_context(nc.Block())
        CONST = 12 * 16
        GROUP_LOAD = 7 * 16

        def wait_apart(eng, waited, count):
            eng.wait_ge(waited, count.v())
            if count.i is not None:
                eng.nop(nofuse=True)

        def loop_of_groups(eng, step, last):
            with eng.Fori(0, last // 2) as i:
                for k in range(2):
                    step(Count(1 + k, i, 2))

        def loop_of_slots(eng, step):
            for s in range(4):
                step(Count(s))
            with eng.Fori(0, SLOT_TILES // 4 - 2) as i:
                for k in range(4):
                    step(Count(4 + k, i, 4))
            for s in range(SLOT_TILES - 4, SLOT_TILES):
                step(Count(s))

        def turn0(g):
            return g * SEQ + SEQ0

        def chunk_turn(u, h):
            return HG * u + h + (u >= 2) + (u >= 5)

        MT1_TURN, MT0_TURN = 2 * HG, 5 * HG + 1

        @block.sync
        def _(sp):
            for b in range(2):
                sp.dma_start(xb[b].rearrange("p (j c) -> p j c", c=C),
                             x[b].rearrange("(j p) c -> p j c", p=P)).then_inc(s_x[b], 16)
            for dst, src in ((ident[:, :], eye), (wq_sb[:, :], Wq), (wk_sb[:, :], Wk), (wv_sb[:, :], Wv),
                             (wo_sb[:, :], Wo), (wr_sb[:, :], Wr), (before_sb[:, :].bitcast(u16), before),
                             (causal_sb[:, :], causal),
                             (bias_qk[:, 0:1], bq.rearrange("(c a) -> c a", a=1)),
                             (bias_qk[:, 1:2], bk.rearrange("(c a) -> c a", a=1)),
                             (bv_row[:, :], bv.rearrange("(a c) -> a c", a=1).to_broadcast([P, C])),
                             (bo_row[:, :], bo.rearrange("(a c) -> a c", a=1).to_broadcast([P, C]))):
                sp.dma_start(dst, src).then_inc(s_const, 16)

            def next_tokens(b):
                sp.wait_ge(s_xc, b - 1)
                sp.dma_start(xb[b % 2].rearrange("p (j c) -> p j c", c=C),
                             x[b].rearrange("(j p) c -> p j c", p=P)).then_inc(s_x[b % 2], 16)

            sp.wait_ge(s_pad, 2)
            for i in range(SLOT_TILES // PAD):
                sp.dma_start(slots[i * PAD * P:(i + 1) * PAD * P, :].rearrange("(j p) c -> p j c", p=P),
                             padrow[:, :, :]).then_inc(s_padded, 16)

            for b in range(B):
                if b + 2 < B:
                    next_tokens(b + 2)
                for s, dst in enumerate((q_split, k_split)):
                    sp.wait_ge(s_part3[s], b + 1)
                    mine = dst[b * NHG:(b + 1) * NHG].rearrange("g h r t -> (g h) r t")
                    for k in range(2 * PARTS - 1 if s == 0 else PARTS):
                        sp.dma_start(mine[:, k * HD:(k + 1) * HD, :],
                                     split[b % 2][:, s, k % PARTS, :]).then_inc(s_split[b % 2], 16)
            for i in range(2):
                sp.wait_ge(s_split[i], 8 * 16 * (B // 2))

            def load(g, hf):
                par = g % 2
                gi = g.v()
                lo = hf * HALF
                done = s_load[par][hf]
                for i in range(PARTS):
                    rows = slice(i * PARTS * HD, (i + 1) * PARTS * HD)
                    sp.dma_start(qs[par][rows, hf, :, :],
                                 q_split[bass.ds(gi, 1), :, i * HD:(i + PARTS) * HD, lo:lo + HALF]
                                 .rearrange("g h r t -> r (g h) t")).then_inc(done, 16)
                    sp.dma_start(ks[par][rows, hf, :, :],
                                 k_split[bass.ds(gi, 1), :, :, lo:lo + HALF]
                                 .rearrange("g h r t -> r (g h) t")).then_inc(done, 16)
                sp.dma_start(ks[par][ROW_ONE:ROW_MAX, hf, :, :].bitcast(u16),
                             alibi[bass.ds(gi, 1), :, :, lo:lo + HALF]
                             .rearrange("g i h t -> i (g h) t")).then_inc(done, 16)

            def place_maxima(g, hf):
                sp.wait_ge(s_mt, (g * 2 + (hf + 1)).v())
                for i in range(PARTS):
                    dst = qs[g % 2][ROW_MAX + i:ROW_MAX + i + 1, hf, :, :].rearrange("p h t -> p (h t)")
                    sp.dma_start(dst.rearrange("p (m t) -> p m t", t=P), mt[hf][:, i, :]).then_inc(s_mrow[hf], 16)

            for stacks, stairs in ((qs, stairs_q), (ks, stairs_k)):
                for par in range(2):
                    sp.dma_start(stacks[par][ROWS:ROWS_DIAG, :, :, :].rearrange("r f h t -> r (f h t)")
                                 .rearrange("r (m t) -> r m t", t=P).bitcast(u16),
                                 stairs.unsqueeze(1).to_broadcast([STEPS, 2 * HG * QT, P])).then_inc(s_stairs, 16)
            sp.wait_ge(s_stack_ones, 4)
            for g in range(2):
                for hf in range(2):
                    load(Count(g), hf)
            place_maxima(Count(0), 0)

            def step(g, loads=True, maxima=True):
                place_maxima(g, 1)
                if maxima:
                    place_maxima(g + 1, 0)
                if loads:
                    sp.wait_ge(s_score, (g * 24 + 16).v())
                    load(g + 2, 0)
                    sp.wait_ge(s_score, (g * 24 + 24).v())
                    load(g + 2, 1)

            step(Count(0))
            loop_of_groups(sp, step, G - 4)
            sp.wait_ge(s_lg_ps, B)
            for e in range(E):
                sp.dma_start(wg_sb[:, e * HID:(e + 1) * HID], Wg[e]).then_inc(s_weights, 16)
                sp.dma_start(wu_sb[:, e * HID:(e + 1) * HID], Wu[e]).then_inc(s_weights, 16)
                sp.dma_start(wd_sb[:, e * HID:(e + 1) * HID].rearrange("p (j c) -> p j c", c=C),
                             Wd[e].rearrange("(j p) c -> p j c", p=P)).then_inc(s_weights, 16)
            step(Count(G - 3))
            step(Count(G - 2), loads=False)
            step(Count(G - 1), loads=False, maxima=False)

            for n in range(NT // QT):
                if n >= 2:
                    sp.wait_ge(s_xbo, n - 1)
                b, hf = divmod(n, 2)
                sp.dma_start(xres[n % 2][:, :].rearrange("p (j c) -> p j c", c=C),
                             x[b, hf * HALF:(hf + 1) * HALF].rearrange("(j p) c -> p j c", p=P)
                             ).then_inc(s_xres[n % 2], 16)

            sp.wait_ge(s_padded, 16 * (SLOT_TILES // PAD))
            for r in range(TOPK):
                sp.wait_ge(s_scatter[r], 16 * NT)

            def rows(s):
                if s.a or s.c >= 4:
                    sp.wait_ge(s_y, (s + -3).v())
                    sp.wait_ge(s_yidx, (s + -3).v())
                at = s.v() * P if s.a == 0 else s.i * (s.a * P) + s.c * P
                sp.dma_start(row_in[s % 4][:, :], slots[bass.ds(at, P), :]).then_inc(s_row[s % 4], 16)

            for s in range(4):
                rows(Count(s))
            with sp.Fori(1, SLOT_TILES // 4) as i:
                for k in range(4):
                    rows(Count(k, i, 4))

            for r in range(TOPK):
                sp.wait_ge(s_routed[r], 16 * (SLOT_TILES // 2))
            for n in range(NT // QT):
                if n >= 2:
                    sp.wait_ge(s_fin, n - 1)
                sp.dma_start(yres[n % 2].rearrange("p (j c) -> p j c", c=TOPK * C),
                             routed[n * QT * P * TOPK:(n + 1) * QT * P * TOPK, :]
                             .rearrange("(j p r) c -> p j (r c)", p=P, r=TOPK)).then_inc(s_yres[n % 2], 16)

        @block.gpsimd
        def _(pool):
            nc.gpsimd.memset(padrow[:, :, :], 0.0).then_inc(s_pad, 1)
            pool.wait_ge(s_pad, 1)
            nc.gpsimd.iota(padrow[:, :, C + 1], pattern=[[P, PAD]], base=N * TOPK, channel_multiplier=1,
                           allow_small_or_imprecise_dtypes=True).then_inc(s_pad, 1)
            nc.gpsimd.memset(ones_bf[:, :], 1.0).then_inc(s_ones, 1)
            for i in range(2):
                nc.gpsimd.memset(vs[i][:, :, :, :], 0.0).then_inc(s_ones, 1)
            pool.wait_ge(s_ones, 3)
            for i in range(2):
                nc.gpsimd.memset(vs[i][:, :, :, HD:HD + 1], 1.0).then_inc(s_ones, 1)
            nc.gpsimd.iota(eidx[:, :], pattern=[[0, NT], [1, E]], base=0, channel_multiplier=0,
                           allow_small_or_imprecise_dtypes=True).then_inc(s_iota, 1)
            nc.gpsimd.iota(tile_no[:, :], pattern=[[1, SLOT_TILES]], base=0, channel_multiplier=0,
                           allow_small_or_imprecise_dtypes=True).then_inc(s_iota, 1)
            nc.gpsimd.iota(meta[:, :, :, 1], pattern=[[TOPK * P, NT], [1, TOPK]], base=0, channel_multiplier=TOPK,
                           allow_small_or_imprecise_dtypes=True).then_inc(s_iota, 1)
            for b in range(B):
                parts = split[b % 2][:, 1]
                pool.wait_ge(s_qk, 4 * b + 4)
                if b:
                    pool.wait_ge(s_part3[1], b)
                nc.gpsimd.tensor_tensor(rest[1], full[1], parts[:, 0, :], ALU.subtract).then_inc(s_rest[1], 1)
                pool.wait_ge(s_rest[1], b + 1)
                nc.gpsimd.tensor_copy(parts[:, 1, :], rest[1]).then_inc(s_part2[1], 1)
                pool.wait_ge(s_part2[1], b + 1)
                nc.gpsimd.tensor_tensor(parts[:, 2, :], rest[1], parts[:, 1, :], ALU.subtract).then_inc(s_part3[1], 1)

            def copy_values(g):
                gi = g.v()
                at = gi * (BT * HG * HD)
                nc.gpsimd.tensor_copy(vs[g % 2][:, :, :, 0:HD].rearrange("p j c d -> p (j c) d"),
                                      vall[:, bass.ds(at, BT * HG * HD)].rearrange("p (m d) -> p m d", d=HD)
                                      ).then_inc(s_vcopy, 1)

            pool.wait_ge(s_v, 2 * B)
            copy_values(Count(0))
            pool.wait_ge(s_meta, 1)
            pool.wait_ge(s_padded, 16 * (SLOT_TILES // PAD))

            def scatter(g, k, r):
                n = g * 2 + k
                gi = g.v()
                if g.a or n.c >= 1:
                    wait_apart(pool, s_scatter[r], n * 16)
                nc.gpsimd.tensor_copy(stage[r][:, 0:C], xn[:, bass.ds(gi * (2 * C) + k * C, C)]).then_inc(s_staged, 1)
                mine = meta[:, bass.ds(gi * 2 + k, 1), r, :].rearrange("p a m -> p (a m)")
                nc.gpsimd.tensor_copy(stage[r][:, C:ROW], mine[:, 0:2]).then_inc(s_staged, 1)
                nc.gpsimd.tensor_copy(stage_idx[r][:, :], mine[:, 2:3]).then_inc(s_staged, 1)
                wait_apart(pool, s_staged, n * 6 + (3 * r + 3))
                pool.indirect_dma_start(slots[:, :], bass.IndirectOffsetOnAxis(ap=stage_idx[r][:, :], axis=0),
                                        stage[r][:, :], None).then_inc(s_scatter[r], 16)

            def step(g, values=True):
                if values:
                    if g.a or g.c:
                        wait_apart(pool, s_pv, g * UNITS)
                    copy_values(g + 1)
                diagonal = 0
                for u in range(UNITS):
                    if prob_unit(u)[3]:
                        diagonal += 1
                        wait_apart(pool, s_exp, g * 24 + (2 * u + 2))
                        first = prob[u % 2][:, :, 0:P]
                        nc.gpsimd.affine_select(out=first, in_=first, compare_op=ALU.is_ge, fill=0.0, base=0,
                                                pattern=[[0, HG], [1, P]], channel_multiplier=-1).then_inc(s_causal, 1)
                    elif u == 4:
                        for k in range(2):
                            for r in range(TOPK):
                                scatter(g, k, r)

            step(Count(0))
            loop_of_groups(pool, step, G - 2)
            step(Count(G - 1), values=False)

            for n in range(NT // QT):
                pool.wait_ge(s_xres[n % 2], 16 * (n // 2 + 1))
                if n >= 2:
                    pool.wait_ge(s_res, n - 1)
                nc.gpsimd.tensor_tensor(xbo[n % 2][:, :].rearrange("p (j c) -> p j c", c=C),
                                        xres[n % 2][:, :].rearrange("p (j c) -> p j c", c=C),
                                        bo_row[:, :].unsqueeze(1).to_broadcast([P, QT, C]), ALU.add).then_inc(s_xbo, 1)

            def put(s):
                pool.wait_ge(s_yidx, (s + 1).v())
                wait_apart(pool, s_y, s + 1)
                pool.indirect_dma_start(routed[:, :], bass.IndirectOffsetOnAxis(ap=y_idx[s % 4][:, :], axis=0),
                                        y_out[s % 2][:, :], None).then_inc(s_routed[s % 2], 16)

            loop_of_slots(pool, put)

        @block.scalar
        def _(act):
            act.wait_ge(s_const, CONST)
            nc.scalar.mul(bias_q_scaled[:, :], bias_qk[:, 0:1], HD ** -0.5).then_inc(s_bias, 1)
            act.wait_ge(s_bias, 1)

            def norm(b):
                act.wait_ge(s_xc, b + 1)
                if b:
                    act.wait_ge(s_var, b)
                nc.scalar.activation(sq, xn[:, b * T:(b + 1) * T], ACT.Square).then_inc(s_sq, 1)
                act.wait_ge(s_var, b + 1)
                if b:
                    act.wait_ge(s_xn, b)
                nc.scalar.activation(stat[:, 2, :], stat[:, 1, :], ACT.Sqrt).then_inc(s_std, 1)

            norm(0)
            for b in range(B):
                for i in range(2):
                    act.wait_ge(s_xt_ps, 2 * b + i + 1)
                    if b >= 2 and i == 0:
                        act.wait_ge(s_lg_ps, b - 1)
                    nc.scalar.copy(xt[b % 2][:, i * HALF:(i + 1) * HALF], ps[:, i, :]).then_inc(s_xt, 1)
                if b + 1 < B:
                    norm(b + 1)
                for s in range(2):
                    act.wait_ge(s_qk_ps, 2 * b + s + 1)
                    if b:
                        act.wait_ge(s_part2[s], b)
                    if b >= 2:
                        act.wait_ge(s_split[b % 2], 8 * 16 * (b // 2))
                    src = ps[:, 2 + 2 * s:4 + 2 * s, :].rearrange("p a t -> p (a t)")
                    bias, scale = (bias_q_scaled[:, :], HD ** -0.5) if s == 0 else (bias_qk[:, 1:2], 1.0)
                    for dst in (full[s], split[b % 2][:, s, 0, :]):
                        nc.scalar.activation(dst, src, ACT.Identity, bias=bias, scale=scale).then_inc(s_qk, 1)

            act.wait_ge(s_gap, 1)
            nc.scalar.activation(rs[:, 4, :], rs[:, 3, :], ACT.Exp).then_inc(s_gap_exp, 1)
            act.wait_ge(s_split[1], 8 * 16 * (B // 2))

            def take_out(g, hf):
                act.wait_ge(s_pv, (g * UNITS + (4 if hf == 0 else UNITS)).v())
                nc.scalar.copy(ot[hf][:, :], ps[:, 6 + hf, :]).then_inc(s_ocopy, 1)

            def step(g):
                for u in range(UNITS):
                    q0 = prob_unit(u)[2]
                    n = HALF - q0
                    if g.a or g.c or u >= 2:
                        act.wait_ge(s_pv, (g * UNITS + (u - 1)).v())
                    for pair in range(2):
                        act.wait_ge(s_score, (g * 24 + (2 * u + pair + 1)).v())
                        nc.scalar.activation(prob[u % 2][:, 2 * pair:2 * pair + 2, 0:n],
                                             ps[:, 2 * pair:2 * pair + 2, 0:n], ACT.Exp).then_inc(s_exp, 1)
                    if u == 0 and (g.a or g.c):
                        take_out(g + -1, 1)
                    if u == 4:
                        take_out(g, 0)

            step(Count(0))
            loop_of_groups(act, step, G - 2)
            step(Count(G - 1))
            take_out(Count(G - 1), 1)

            for n in range(NT // QT):
                act.wait_ge(s_at_ps, n + 1)
                if n >= 2:
                    act.wait_ge(s_wo, n - 1)
                nc.scalar.copy(at_sb[n % 2][:, :], ps[:, n % 2, :]).then_inc(s_at, 1)

            def copy_row(s):
                act.wait_ge(s_row_ps, (s + 1).v())
                nc.scalar.copy(row_t[s % 2][:, :], ps[:, 4 + s % 2, 0:P]).then_inc(s_row_t, 1)

            def silu(s):
                act.wait_ge(s_gate_ps, (s + 1).v())
                if s.a or s.c >= 2:
                    act.wait_ge(s_hid, (s + -1).v())
                nc.scalar.activation(gate[s % 2][:, :], ps[:, s % 2, :], ACT.Silu).then_inc(s_gate, 1)

            def weigh(s):
                act.wait_ge(s_y_ps, (s + 1).v())
                if s.a or s.c >= 2:
                    act.wait_ge(s_routed[s % 2], (s // 2 * 16).v())
                nc.scalar.activation(y_out[s % 2][:, :], ps[:, 4 + s % 2, P:2 * P], ACT.Copy,
                                     scale=row_in[s % 4][:, C:C + 1]).then_inc(s_y, 1)

            act.wait_ge(s_res, NT // QT)
            copy_row(Count(0))
            silu(Count(0))
            copy_row(Count(1))

            def expert(s):
                peeled = not s.a
                if not peeled or s.c + 1 < SLOT_TILES:
                    silu(s + 1)
                if not peeled or s.c >= 1:
                    weigh(s + -1)
                if not peeled or s.c + 2 < SLOT_TILES:
                    copy_row(s + 2)

            loop_of_slots(act, expert)
            weigh(Count(SLOT_TILES - 1))
            for n in range(NT // QT):
                act.wait_ge(s_fin, n + 1)
                b, hf = divmod(n, 2)
                act.dma_start(out[b, hf * HALF:(hf + 1) * HALF].rearrange("(j p) c -> p j c", p=P),
                              fin[n % 2].rearrange("p (j c) -> p j c", c=C)).then_inc(s_out[n % 2], 16)
            for i in range(2):
                act.wait_ge(s_out[i], 16 * (NT // QT // 2))

        @block.vector
        def _(dve):
            chain = [0]

            def link(ins):
                chain[0] += 1
                ins.then_inc(s_ln, 1)
                dve.wait_ge(s_ln, chain[0])

            for i in range(2):
                nc.vector.memset(qs[i][64:ROWS, :, :, :], 1.0).then_inc(s_stack_ones, 1)
                nc.vector.memset(ks[i][64:ROWS, :, :, :], 1.0).then_inc(s_stack_ones, 1)

            inv, var, std, r, t = [stat[:, i, :] for i in range(5)]

            def col(a):
                return a.unsqueeze(2).to_broadcast([P, BT, C])

            def tiles(a):
                return a.rearrange("p (j c) -> p j c", c=C)

            def norm(b):
                dve.wait_ge(s_x[b % 2], 16 * (b // 2 + 1))
                link(nc.vector.tensor_reduce(inv, tiles(xb[b % 2]), AX.X, ALU.add))
                link(nc.vector.tensor_scalar(t, inv, 1.0 / C, None, ALU.mult))
                mine = tiles(xn[:, b * T:(b + 1) * T])
                nc.vector.tensor_tensor(mine, tiles(xb[b % 2]), col(t), ALU.subtract).then_inc(s_xc, 1)
                dve.wait_ge(s_sq, b + 1)
                link(nc.vector.tensor_reduce(inv, tiles(sq), AX.X, ALU.add))
                nc.vector.tensor_scalar(var, inv, 1.0 / C, EPS, ALU.mult, ALU.add).then_inc(s_var, 1)
                dve.wait_ge(s_var, b + 1)
                dve.wait_ge(s_std, b + 1)
                link(nc.vector.reciprocal(r, std))
                link(nc.vector.tensor_tensor(t, r, r, ALU.mult))
                link(nc.vector.tensor_tensor(t, t, var, ALU.mult))
                link(nc.vector.tensor_scalar(t, t, -0.5, 1.5, ALU.mult, ALU.add))
                link(nc.vector.tensor_tensor(t, t, r, ALU.mult))
                nc.vector.tensor_tensor(mine, mine, col(t), ALU.mult).then_inc(s_xn, 1)

            def split_queries(b):
                parts = split[b % 2][:, 0]
                dve.wait_ge(s_qk, 4 * b + 2)
                nc.vector.tensor_tensor(rest[0], full[0], parts[:, 0, :], ALU.subtract).then_inc(s_rest[0], 1)
                dve.wait_ge(s_rest[0], b + 1)
                nc.vector.tensor_copy(parts[:, 1, :], rest[0]).then_inc(s_part2[0], 1)
                dve.wait_ge(s_part2[0], b + 1)
                nc.vector.tensor_tensor(parts[:, 2, :], rest[0], parts[:, 1, :], ALU.subtract).then_inc(s_part3[0], 1)

            def values(b):
                dve.wait_ge(s_v_ps, b + 1)
                dst = vall[:, b * T:(b + 1) * T].rearrange("p (g j c) -> p j g c", g=NHG, j=BT)
                for i in range(2):
                    for j in range(4):
                        last = nc.vector.tensor_tensor(
                            dst[:, 4 * i + j],
                            ps[:, 6 + i, j * P:(j + 1) * P].rearrange("p (g c) -> p g c", g=NHG),
                            bv_row[:, :].rearrange("p (g c) -> p g c", g=NHG), ALU.add)
                    last.then_inc(s_v, 1)
                dve.wait_ge(s_lg_ps, b + 1)
                nc.vector.tensor_copy(logits[:, b * BT * E:(b + 1) * BT * E], ps[:, 0, 0:BT * E]).then_inc(s_lg, 1)

            norm(0)
            dve.wait_ge(s_const, CONST)
            for b in range(B):
                if b + 1 < B:
                    norm(b + 1)
                split_queries(b)
                values(b)

            def by_token(a):
                return a.rearrange("p (n e) -> p n e", e=E)

            def over_e(a):
                return a.unsqueeze(2).to_broadcast([P, NT, E])

            hit, pick1, pick2, masked, work, pos = [by_token(a[:, :]) for a in rt]
            lg, ei = by_token(logits[:, :]), by_token(eidx[:, :])
            v1, v2, idx, gap, egap = [rs[:, i, :] for i in range(5)]
            dve.wait_ge(s_lg, B)
            dve.wait_ge(s_iota, 3)

            def top(values, best, pick):
                link(nc.vector.tensor_reduce(best, values, AX.X, ALU.max))
                link(nc.vector.tensor_tensor(hit, values, over_e(best), ALU.is_equal))
                link(nc.vector.scalar_tensor_tensor(work, hit, -float(E), ei, ALU.mult, ALU.add))
                link(nc.vector.tensor_reduce(idx, work, AX.X, ALU.min))
                link(nc.vector.tensor_scalar(idx, idx, float(E), None, ALU.add))
                link(nc.vector.tensor_tensor(pick, ei, over_e(idx), ALU.is_equal))

            top(lg, v1, pick1)
            link(nc.vector.scalar_tensor_tensor(masked, pick1, NEG, lg, ALU.mult, ALU.add))
            top(masked, v2, pick2)
            nc.vector.tensor_tensor(gap, v2, v1, ALU.subtract).then_inc(s_gap, 1)
            nc.vector.tensor_tensor(by_token(mask_bf[:, :]), pick1, pick2, ALU.add).then_inc(s_mask, 1)
            dve.wait_ge(s_gap_exp, 1)
            link(nc.vector.tensor_scalar(v1, egap, 1.0, None, ALU.add))
            link(nc.vector.reciprocal(v2, v1))
            link(nc.vector.tensor_scalar(v2, v2, float(DEPTH_SCALE), None, ALU.mult))
            nc.vector.tensor_copy(meta[:, :, 0, 0], v2)
            link(nc.vector.tensor_tensor(meta[:, :, 1, 0], v2, egap, ALU.mult))
            dve.wait_ge(s_count, 1)
            counts, upto, start = rt[3][:, :], rt[4][:, :], rt[0][:, :]
            ones_row = rt[5][:, :]
            link(nc.vector.memset(ones_row, 1.0))
            link(nc.vector.tensor_copy(counts.rearrange("p (e n) -> p e n", e=E),
                                       ps[:, 1, 0:NT * E].rearrange("p (n e) -> p e n", e=E)))
            link(nc.vector.tensor_tensor_scan(upto, ones_row, counts, 0.0, ALU.mult, ALU.add))
            link(nc.vector.tensor_tensor(start, upto, counts, ALU.subtract))
            by_e = [a.rearrange("p (e n) -> p e n", e=E) for a in (upto, start)]
            link(nc.vector.tensor_tensor(ex[:, 0, :], by_e[0][:, :, NT - 1], by_e[1][:, :, 0], ALU.subtract))
            link(nc.vector.tensor_scalar(exi[:, 0, :], ex[:, 0, :], float(P - 1), None, ALU.add))
            link(nc.vector.tensor_scalar(exi[:, 1, :], exi[:, 0, :], int(np.log2(P)), None, ALU.logical_shift_right))
            link(nc.vector.tensor_copy(ex[:, 1, :], exi[:, 1, :]))
            link(nc.vector.tensor_tensor_scan(ex[:, 2, :], ones_row[:, 0:E], ex[:, 1, :], 0.0, ALU.mult, ALU.add))
            link(nc.vector.tensor_tensor(ex[:, 3, :], ex[:, 2, :], ex[:, 1, :], ALU.subtract))
            link(nc.vector.scalar_tensor_tensor(ex[:, 4, :], ex[:, 3, :], float(P), by_e[1][:, :, 0],
                                                ALU.mult, ALU.subtract))
            link(nc.vector.tensor_tensor(by_token(counts), by_e[1].rearrange("p e n -> p n e"),
                                         by_token(ps[:, 0, 0:NT * E]), ALU.add))
            link(nc.vector.tensor_tensor(pos, by_token(counts),
                                         ex[:, 4, :].unsqueeze(1).to_broadcast([P, NT, E]), ALU.add))
            for k, pick in enumerate((pick1, pick2)):
                link(nc.vector.tensor_tensor(work, pick, pos, ALU.mult))
                last = nc.vector.tensor_reduce(meta[:, :, k, 2], work, AX.X, ALU.add)
                if k == 0:
                    link(last)
            last.then_inc(s_meta, 1)
            own = owner[:, :].rearrange("p (n e) -> p n e", e=E)
            link(nc.vector.tensor_tensor(own, ex[0:1, 2, :].unsqueeze(1).to_broadcast([1, SLOT_TILES, E]),
                                         tile_no[:, :].unsqueeze(2).to_broadcast([1, SLOT_TILES, E]), ALU.is_le))
            link(nc.vector.tensor_reduce(owner_f[:, :], own, AX.X, ALU.add))
            nc.vector.tensor_scalar(owner_i[:, :], owner_f[:, :], float(E - 1), None, ALU.min).then_inc(s_owner, 1)

            def read_chunk(g, turn, u, h):
                qt, kh, n, diagonal = max_unit(u)
                dst = mx_late[:, :] if kh else mx[:, qt // QT, :]
                dst = dst[:, h * QT + qt % QT:h * QT + qt % QT + 1]
                src = ps[:, 4 + turn % 2, 0:n]
                if diagonal:
                    wait_apart(dve, s_chunk, turn + 1)
                else:
                    dve.wait_ge(s_chunk, (turn + 1).v())
                if diagonal:
                    ins = nc.vector.tensor_tensor_reduce(out=junk[turn % 2][:, 0:n], in0=src, in1=causal_sb[:, HALF - n:HALF],
                                                         scale=1.0, scalar=NEG, op0=ALU.add, op1=ALU.max,
                                                         accum_out=dst)
                else:
                    ins = nc.vector.tensor_reduce(dst, src, AX.X, ALU.max)
                ins.then_inc(s_read, 1)

            def join_maxima(g, turn):
                dve.wait_ge(s_read, turn.v())
                nc.vector.tensor_tensor(mx_all[:, :], mx[:, 1, :], mx_late[:, :], ALU.max).then_inc(s_mx, 1)

            def split_maxima(g, hf, turn):
                event = g * 2 + hf
                dve.wait_ge(s_chunk, (turn + 1).v())
                if g.a or g.c:
                    dve.wait_ge(s_mrow[hf], (g * (PARTS * 16)).v())
                src = ps[0:HG * QT, 4 + turn % 2, 0:P]
                dst = mt[hf]
                nc.vector.tensor_scalar(dst[:, 0, :], src, -1.0, None, ALU.mult).then_inc(s_mpart, 1)
                dve.wait_ge(s_mpart, (event * 2 + 1).v())
                nc.vector.scalar_tensor_tensor(mrest[:, :], src, -1.0, dst[:, 0, :], ALU.mult,
                                               ALU.subtract).then_inc(s_read, 1)
                dve.wait_ge(s_read, (turn + 1).v())
                nc.vector.tensor_copy(dst[:, 1, :], mrest[:, :]).then_inc(s_mpart, 1)
                dve.wait_ge(s_mpart, (event * 2 + 2).v())
                nc.vector.tensor_tensor(dst[:, 2, :], mrest[:, :], dst[:, 1, :], ALU.subtract).then_inc(s_mt, 1)

            def divide(g, hf):
                dve.wait_ge(s_ot, (g * 2 + (hf + 1)).v())
                src = ps[:, 6 + hf, :].rearrange("p (m w) -> p m w", w=32)
                nc.vector.reciprocal(rden[:, hf, :], src[:, :, HD]).then_inc(s_rden, 1)
                dve.wait_ge(s_rden, (g * 2 + (hf + 1)).v())
                at = g.v() * (BT * HG * HD) + hf * P
                nc.vector.tensor_tensor(attn[:, bass.ds(at, P)].rearrange("p (m d) -> p m d", d=HD),
                                        src[:, :, 0:HD],
                                        rden[:, hf, :].unsqueeze(2).to_broadcast([P, HG * QT, HD]),
                                        ALU.mult).then_inc(s_norm, 1)

            for u in range(UNITS):
                for h in range(HG):
                    read_chunk(Count(0), Count(HG * u + h), u, h)
            join_maxima(Count(0), Count(UNITS * HG))
            split_maxima(Count(0), 0, Count(UNITS * HG))

            def step(g, ahead=True):
                turn = turn0(g)
                for u in range(UNITS):
                    if ahead:
                        for h in range(HG):
                            read_chunk(g + 1, turn + chunk_turn(u, h), u, h)
                    if u == 1:
                        split_maxima(g, 1, turn + (MT1_TURN if ahead else 0))
                    if u == 2 and (g.a or g.c):
                        divide(g + -1, 1)
                    if u == 4 and ahead:
                        split_maxima(g + 1, 0, turn + MT0_TURN)
                    if u == 6:
                        divide(g, 0)
                if ahead:
                    join_maxima(g + 1, turn + SEQ)

            step(Count(0))
            loop_of_groups(dve, step, G - 2)
            step(Count(G - 1), ahead=False)
            divide(Count(G - 1), 1)

            for r in range(TOPK):
                dve.wait_ge(s_scatter[r], 16 * NT)
            dve.wait_ge(s_norm, 2 * G)

            def gather_heads(n):
                b, hf = divmod(n, 2)
                if n >= 2:
                    dve.wait_ge(s_at_ps, n - 1)
                src = attn[:, b * T:(b + 1) * T].rearrange("p (g j c) -> p j g c", g=NHG, j=BT)
                dst = heads[n % 2][:, :].rearrange("p (j g c) -> p j g c", j=QT, g=NHG)
                nc.vector.tensor_copy(dst, src[:, hf * QT:(hf + 1) * QT]).then_inc(s_heads, 1)

            gather_heads(0)
            for n in range(NT // QT):
                if n + 1 < NT // QT:
                    gather_heads(n + 1)
                dve.wait_ge(s_wo, n + 1)
                dve.wait_ge(s_xbo, n + 1)
                nc.vector.tensor_tensor(xn[:, n * HALF:(n + 1) * HALF], ps[:, 2 + n % 2, :], xbo[n % 2][:, :],
                                        ALU.add).then_inc(s_res, 1)

            def multiply(s):
                dve.wait_ge(s_gate, (s + 1).v())
                dve.wait_ge(s_up_ps, (s + 1).v())
                if s.a or s.c >= 2:
                    dve.wait_ge(s_hid_ps, (s + -1).v())
                nc.vector.tensor_tensor(hid[s % 2][:, :], ps[:, 2 + s % 2, :], gate[s % 2][:, :],
                                        ALU.mult).then_inc(s_hid, 1)

            def expert(s):
                peeled = not s.a
                if not peeled or s.c + 1 < SLOT_TILES:
                    multiply(s + 1)
                dve.wait_ge(s_hid_ps, (s + 1).v())
                if not peeled or s.c >= 2:
                    dve.wait_ge(s_y_ps, (s + -1).v())
                nc.vector.tensor_copy(hid_t[s % 2][:, :], ps[:, 6 + s % 2, :]).then_inc(s_hid_t, 1)
                dve.wait_ge(s_row[s % 4], (s // 4 * 16 + 16).v())
                if not peeled or s.c >= 4:
                    dve.wait_ge(s_routed[s % 2], (s // 2 * 16 + -16).v())
                nc.vector.tensor_copy(y_idx[s % 4][:, :], row_in[s % 4][:, C + 1:C + 2]).then_inc(s_yidx, 1)

            multiply(Count(0))
            loop_of_slots(dve, expert)

            for n in range(NT // QT):
                dve.wait_ge(s_yres[n % 2], 16 * (n // 2 + 1))
                y = yres[n % 2].rearrange("p (j r c) -> p j r c", r=TOPK, c=C)
                mine = tiles(xn[:, n * HALF:(n + 1) * HALF])
                nc.vector.tensor_tensor(mine, mine, y[:, :, 0, :], ALU.add).then_inc(s_acc, 1)
                dve.wait_ge(s_acc, n + 1)
                if n >= 2:
                    dve.wait_ge(s_out[n % 2], 16 * (n // 2))
                nc.vector.tensor_tensor(tiles(fin[n % 2]), mine, y[:, :, 1, :], ALU.add).then_inc(s_fin, 1)

        @block.tensor
        def _(pe):
            pe.wait_ge(s_const, CONST)
            for b in range(B):
                pe.wait_ge(s_xn, b + 1)
                if b:
                    pe.wait_ge(s_xt, 2 * b)
                    pe.wait_ge(s_lg, b)
                for j in range(BT):
                    last = nc.tensor.transpose(ps[:, j // 4, (j % 4) * P:(j % 4 + 1) * P],
                                               xn[:, b * T + j * C:b * T + (j + 1) * C], ident[:, :])
                    if j % 4 == 3:
                        last.then_inc(s_xt_ps, 1)
                pe.wait_ge(s_xt, 2 * b + 2)
                for s, w in enumerate((wq_sb, wk_sb)):
                    if b:
                        pe.wait_ge(s_qk, 4 * (b - 1) + 2 * s + 2)
                    for i in range(2):
                        last = nc.tensor.matmul(ps[:, 2 + 2 * s + i, :], w[:, :],
                                                xt[b % 2][:, i * HALF:(i + 1) * HALF], start=True, stop=True)
                    last.then_inc(s_qk_ps, 1)
                if b:
                    pe.wait_ge(s_v, 2 * b)
                for j in range(BT):
                    last = nc.tensor.matmul(ps[:, 6 + j // 4, (j % 4) * P:(j % 4 + 1) * P],
                                            xt[b % 2][:, j * P:(j + 1) * P], wv_sb[:, :], start=True, stop=True)
                last.then_inc(s_v_ps, 1)
                for j in range(BT):
                    last = nc.tensor.matmul(ps[:, 0, j * E:(j + 1) * E], xt[b % 2][:, j * P:(j + 1) * P],
                                            wr_sb[:, :], start=True, stop=True)
                last.then_inc(s_lg_ps, 1)

            pe.wait_ge(s_mask, 1)
            pe.wait_ge(s_ones, 1)
            nc.tensor.matmul(ps[:, 0, 0:NT * E], before_sb[:, :], mask_bf[:, :], start=True, stop=True)
            nc.tensor.matmul(ps[:, 1, 0:NT * E], ones_bf[:, :], mask_bf[:, :], start=True, stop=True
                             ).then_inc(s_count, 1)

            def chunk(g, turn, u, h):
                qt, kh, n, _ = max_unit(u)
                if turn.a or turn.c >= 2:
                    pe.wait_ge(s_read, (turn + -1).v())
                nc.tensor.matmul(ps[:, 4 + turn % 2, 0:n],
                                 qs[g % 2][0:ROW_MAX, qt // QT, h, (qt % QT) * P:(qt % QT + 1) * P],
                                 ks[g % 2][0:ROW_MAX, kh, h, 0:n], start=True, stop=True).then_inc(s_chunk, 1)

            def wait_stacks(g, u):
                if u in (0, 4):
                    pe.wait_ge(s_load[g % 2][u // 4], (g // 2 * GROUP_LOAD + GROUP_LOAD).v())

            def transpose_maxima(src, turn):
                pe.wait_ge(s_read, (turn + -1).v())
                nc.tensor.transpose(ps[0:HG * QT, 4 + turn % 2, 0:P], src, ident[:, :]).then_inc(s_chunk, 1)

            def scores(g, u, pair):
                hf, kt, q0, diagonal = prob_unit(u)
                if pair == 0 and u in (0, 4):
                    pe.wait_ge(s_mrow[u // 4], (g * (PARTS * 16) + PARTS * 16).v())
                if g.a or g.c or u:
                    pe.wait_ge(s_exp, (g * 24 + (2 * u + pair - 1)).v())
                pieces = [(ROWS_DIAG, q0, q0 + P)] * diagonal + [(ROWS, q0 + P * diagonal, HALF)]
                for h in (2 * pair, 2 * pair + 1):
                    for rows, lo, hi in pieces:
                        if lo < hi:
                            last = nc.tensor.matmul(ps[:, h, lo - q0:hi - q0],
                                                    ks[g % 2][0:rows, kt // QT, h, (kt % QT) * P:(kt % QT + 1) * P],
                                                    qs[g % 2][0:rows, hf, h, lo:hi], start=True, stop=True)
                last.then_inc(s_score, 1)

            def products(g, u):
                hf, kt, q0, diagonal = prob_unit(u)
                if diagonal:
                    pe.wait_ge(s_causal, (g * 8 + (u + 1 if u < 4 else u - 3)).v())
                else:
                    pe.wait_ge(s_exp, (g * 24 + (2 * u + 2)).v())
                if u == 0:
                    pe.wait_ge(s_vcopy, (g + 1).v())
                if u in (0, 4) and (g.a or g.c):
                    pe.wait_ge(s_norm, (g * 2 + (-1 if u == 0 else 0)).v())
                for h in range(HG):
                    last = nc.tensor.matmul(ps[32 * h:32 * h + 32, 6 + hf, q0:HALF], vs[g % 2][:, kt, h, :],
                                            prob[u % 2][:, h, 0:HALF - q0], start=(kt == 0),
                                            stop=(kt == (QT - 1 if hf == 0 else BT - 1)))
                last.then_inc(s_pv, 1)

            def transpose_result(g, hf):
                pe.wait_ge(s_ocopy, (g * 2 + (hf + 1)).v())
                for j in range(QT):
                    last = nc.tensor.transpose(ps[:, 6 + hf, j * P:(j + 1) * P], ot[hf][:, j * P:(j + 1) * P],
                                               ident[:, :])
                last.then_inc(s_ot, 1)

            pe.wait_ge(s_ones, 5)
            pe.wait_ge(s_stairs, 4 * 16)
            for u in range(UNITS):
                wait_stacks(Count(0), u)
                for h in range(HG):
                    chunk(Count(0), Count(HG * u + h), u, h)
            pe.wait_ge(s_read, 4 * HG)
            transpose_maxima(mx[:, 0, :], Count(UNITS * HG))
            pe.wait_ge(s_meta, 1)
            for pair in range(2):
                scores(Count(0), 0, pair)

            def step(g, ahead=True):
                turn = turn0(g)
                for u in range(UNITS):
                    for pair in range(2):
                        if u + 1 < UNITS:
                            scores(g, u + 1, pair)
                        elif ahead:
                            scores(g + 1, 0, pair)
                        if ahead:
                            if pair == 0:
                                wait_stacks(g + 1, u)
                            for h in (2 * pair, 2 * pair + 1):
                                chunk(g + 1, turn + chunk_turn(u, h), u, h)
                    if u == 1:
                        pe.wait_ge(s_mx, (g + 1).v())
                        transpose_maxima(mx_all[:, :], turn + (MT1_TURN if ahead else 0))
                    if u == 2 and (g.a or g.c):
                        transpose_result(g + -1, 1)
                    if u == 4 and ahead:
                        pe.wait_ge(s_read, (turn + (chunk_turn(3, HG - 1) + 1)).v())
                        transpose_maxima(mx[:, 0, :], turn + MT0_TURN)
                    if u == 6:
                        transpose_result(g, 0)
                    products(g, u)

            step(Count(0))
            loop_of_groups(pe, step, G - 2)
            step(Count(G - 1), ahead=False)
            transpose_result(Count(G - 1), 1)

            for n in range(NT // QT):
                if n == 0:
                    pe.wait_ge(s_exp, 24 * G)
                if n >= 2:
                    pe.wait_ge(s_at, n - 1)
                pe.wait_ge(s_heads, n + 1)
                for j in range(QT):
                    last = nc.tensor.transpose(ps[:, n % 2, j * P:(j + 1) * P], heads[n % 2][:, j * P:(j + 1) * P],
                                               ident[:, :])
                last.then_inc(s_at_ps, 1)
                pe.wait_ge(s_at, n + 1)
                if n >= 2:
                    pe.wait_ge(s_res, n - 1)
                for j in range(QT):
                    last = nc.tensor.matmul(ps[:, 2 + n % 2, j * P:(j + 1) * P],
                                            at_sb[n % 2][:, j * P:(j + 1) * P], wo_sb[:, :], start=True, stop=True)
                last.then_inc(s_wo, 1)

            pe.wait_ge(s_owner, 1)
            pe.wait_ge(s_weights, 3 * E * 16)
            pe.wait_ge(s_res, NT // QT)

            def expert_of(s):
                return pe.value_load(owner_i[0:1, bass.ds(s.v(), 1)], min_val=0, max_val=E - 1)

            def transpose_row(s):
                pe.wait_ge(s_row[s % 4], (s // 4 * 16 + 16).v())
                if s.a or s.c >= 2:
                    pe.wait_ge(s_row_t, (s + -1).v())
                nc.tensor.transpose(ps[:, 4 + s % 2, 0:P], row_in[s % 4][:, 0:C], ident[:, :]).then_inc(s_row_ps, 1)

            def gate_up(s):
                e = expert_of(s)
                pe.wait_ge(s_row_t, (s + 1).v())
                if s.a or s.c >= 2:
                    pe.wait_ge(s_hid, (s + -1).v())
                nc.tensor.matmul(ps[:, s % 2, :], row_t[s % 2][:, :], wg_sb[:, bass.ds(e * HID, HID)],
                                 start=True, stop=True).then_inc(s_gate_ps, 1)
                nc.tensor.matmul(ps[:, 2 + s % 2, :], row_t[s % 2][:, :], wu_sb[:, bass.ds(e * HID, HID)],
                                 start=True, stop=True).then_inc(s_up_ps, 1)

            def transpose_hidden(s):
                pe.wait_ge(s_hid, (s + 1).v())
                if s.a or s.c >= 2:
                    pe.wait_ge(s_hid_t, (s + -1).v())
                for j in range(HC):
                    last = nc.tensor.transpose(ps[:, 6 + s % 2, j * P:(j + 1) * P],
                                               hid[s % 2][:, j * P:(j + 1) * P], ident[:, :])
                last.then_inc(s_hid_ps, 1)

            def down(s):
                e = expert_of(s)
                pe.wait_ge(s_hid_t, (s + 1).v())
                if s.a or s.c >= 2:
                    pe.wait_ge(s_y, (s + -1).v())
                for j in range(HC):
                    last = nc.tensor.matmul(ps[:, 4 + s % 2, P:2 * P], hid_t[s % 2][:, j * P:(j + 1) * P],
                                            wd_sb[:, bass.ds(e * HID + j * C, C)], start=(j == 0), stop=(j == HC - 1))
                last.then_inc(s_y_ps, 1)

            transpose_row(Count(0))
            gate_up(Count(0))
            transpose_row(Count(1))

            def expert(s):
                peeled = not s.a
                if not peeled or s.c + 1 < SLOT_TILES:
                    gate_up(s + 1)
                transpose_hidden(s)
                if not peeled or s.c >= 1:
                    down(s + -1)
                if not peeled or s.c + 2 < SLOT_TILES:
                    transpose_row(s + 2)

            loop_of_slots(pe, expert)
            down(Count(SLOT_TILES - 1))


_INS = ['L0_attn_x', 'L0_attn_Wq', 'L0_attn_bq', 'L0_attn_Wk', 'L0_attn_bk', 'L0_attn_Wv', 'L0_attn_bv',
        'L0_attn_Wo', 'L0_attn_bo', 'L0_ffn_Wr', 'L0_ffn_Wg', 'L0_ffn_Wu', 'L0_ffn_Wd']


def kernel(**inputs):
    import numpy as _np
    import concourse.bacc as _bacc
    from concourse import mybir as _mybir
    from concourse.bass_utils import run_bass_kernel_spmd as _run

    nc = _bacc.Bacc("TRN2", target_bir_lowering=False, num_devices=1)
    arrays, args = {}, []
    for name in _INS:
        a = _np.ascontiguousarray(inputs[name])
        arrays[f"in_{name}"] = a
        args.append(nc.dram_tensor(f"in_{name}", a.shape, _mybir.dt.from_np(a.dtype), kind="ExternalInput").ap())
    out = nc.dram_tensor("out_0", (B, T, C), _mybir.dt.float32, kind="ExternalOutput").ap()
    build(nc, *args, out)
    r = _run(nc, [arrays], core_ids=[0])
    return r.results[0]["out_0"]
```

```python
import numpy as np
import concourse.bass as bass
from concourse import mybir
from contextlib import ExitStack

fp32 = mybir.dt.float32
bf16 = mybir.dt.bfloat16
i32 = mybir.dt.int32
u32 = mybir.dt.uint32
u16 = mybir.dt.uint16
ALU = mybir.AluOpType
ACT = mybir.ActivationFunctionType
AX = mybir.AxisListType

P = 128
B, T, C = 4, 1024, 128
H, HD = 16, 8
N = B * T
NT = N // P
BT = T // P
HG = 4
NHG = H // HG
G = B * NHG
HALF = T // 2
QT = HALF // P
PARTS = 3
SPLIT = PARTS * PARTS * HD
ROW_ONE = SPLIT
ROW_ZERO = ROW_ONE + PARTS
ROW_MAX = 99
ROWS = ROW_MAX + PARTS
STEP = 5
STEPS = (P - 1) // STEP
ROWS_DIAG = ROWS + STEPS
E, TOPK, HID = 8, 2, 512
HC = HID // P
SLOT_TILES = N * TOPK // P + E
ROW = C + 2
PAD = 8
NEG = -3.0e38
EPS = 1e-5
DEPTH_SCALE = 1.0 / np.sqrt(12)

UNITS = 12
SEQ0 = UNITS * HG + 1
SEQ = UNITS * HG + 2


class Count:

    def __init__(self, c, i=None, a=0):
        self.c, self.i, self.a = c, i, a

    def __add__(self, k):
        return Count(self.c + k, self.i, self.a)

    def __mul__(self, k):
        return Count(self.c * k, self.i, self.a * k)

    def __floordiv__(self, k):
        assert self.a % k == 0
        return Count(self.c // k, self.i, self.a // k)

    def __mod__(self, k):
        assert self.a % k == 0
        return self.c % k

    def v(self):
        return self.c if self.i is None else self.i * self.a + self.c


def max_unit(u):
    if u < 4:
        return u, 0, P * (u + 1), True
    if u < 8:
        return u, 0, HALF, False
    return u - 4, 1, P * (u - 7), True


def prob_unit(u):
    if u < 4:
        return 0, u, P * u, True
    if u < 8:
        return 1, u - 4, 0, False
    return 1, u - 4, P * (u - 8), True


def truncated_parts(a):
    parts, rest = [], a.astype(np.float32)
    for _ in range(PARTS):
        bits = rest.view(np.uint32) & np.uint32(0xFFFF0000)
        parts.append((bits >> 16).astype(np.uint16))
        rest = rest - bits.view(np.float32)
    return parts


def constants(nc):
    start = 2.0 ** (-2.0 ** -(np.log2(H) - 3))
    slopes = np.array([start * start ** i for i in range(H)], np.float32)
    bias = -slopes[:, None] * (T - 1 - np.arange(T, dtype=np.float32))[None, :]
    parts = np.stack(truncated_parts(bias), 1)
    parts = parts.reshape(NHG, HG, PARTS, T).transpose(0, 2, 1, 3)
    alibi = np.tile(parts, (B, 1, 1, 1))
    i = np.arange(P)
    causal = np.zeros((P, HALF), np.float32)
    causal[:, HALF - P:] = np.where(i[None, :] <= i[:, None], 0.0, NEG)
    edge = STEP * (1 + np.arange(STEPS))[:, None]
    fixed_q, fixed_k = np.zeros((2, ROWS_DIAG - ROW_ONE, P), np.uint16)
    one, huge = 0x3F80, 0xF149
    fixed_q[:PARTS] = one
    fixed_q[ROWS - ROW_ONE:] = np.where(i[None, :] < edge, one, 0)
    fixed_k[ROW_MAX - ROW_ONE:ROWS - ROW_ONE] = one
    fixed_k[ROWS - ROW_ONE:] = np.where(i[None, :] >= edge, huge, 0)
    before = np.where(i[:, None] < i[None, :], 0x3F80, 0).astype(np.uint16)
    return (nc.inline_tensor(np.ascontiguousarray(alibi), name="alibi_parts"),
            nc.inline_tensor(np.eye(P, dtype=np.float32), name="identity"),
            nc.inline_tensor(causal, name="causal_bias"),
            nc.inline_tensor(before, name="before_in_tile"),
            nc.inline_tensor(fixed_q, name="fixed_q"), nc.inline_tensor(fixed_k, name="fixed_k"))


def build(nc, x, Wq, bq, Wk, bk, Wv, bv, Wo, bo, Wr, Wg, Wu, Wd, out):
    alibi, eye, causal, before, fixed_q, fixed_k = [t.ap() for t in constants(nc)]
    q_split = nc.dram_tensor("q_split", [G, HG, (2 * PARTS - 1) * HD, T], bf16).ap()
    k_split = nc.dram_tensor("k_split", [G, HG, PARTS * HD, T], bf16).ap()
    slots = nc.dram_tensor("slots", [SLOT_TILES * P, ROW], fp32).ap()
    routed = nc.dram_tensor("routed", [N * TOPK + PAD * P, C], fp32).ap()

    ctx = ExitStack()
    with ctx:
        def sb(name, shape, dt=fp32):
            return ctx.enter_context(nc.sbuf_tensor(name, shape, dt))

        def sem(name):
            return ctx.enter_context(nc.semaphore(name))

        def sems(name, n=2):
            return [sem(f"{name}{i}") for i in range(n)]

        ps = ctx.enter_context(nc.psum_tensor("ps", [P, 8, HALF], fp32))

        xn = sb("xn", [P, NT * C])
        vall = sb("vall", [P, G * BT * HG * HD])
        attn = sb("attn", [P, G * BT * HG * HD])
        weights = sb("weights", [P, E * 3 * HID])
        wg_sb = weights[:, 0:E * HID]
        wu_sb = weights[:, E * HID:2 * E * HID]
        wd_sb = weights[:, 2 * E * HID:3 * E * HID]
        xb = [weights[:, 0:T], weights[:, T:2 * T]]
        sq = weights[:, 2 * T:3 * T]
        xt = [weights[:, 3 * T:4 * T], weights[:, 4 * T:5 * T]]
        full = [weights[:, 5 * T:6 * T], weights[:, 6 * T:7 * T]]
        rest = [weights[:, 7 * T:8 * T], weights[:, 8 * T:9 * T]]
        prob_sb = sb("prob_sb", [P, 2 * HG * HALF])
        prob = [prob_sb[:, i * HG * HALF:(i + 1) * HG * HALF].rearrange("p (c t) -> p c t", c=HG) for i in range(2)]
        split = [a.bitcast(bf16).rearrange("p (s i t) -> p s i t", s=2, i=PARTS)
                 for a in (weights[:, 9 * T:12 * T], prob_sb[:, 0:3 * T])]
        qs = [sb(f"qs{i}", [ROWS_DIAG, 2, HG, HALF], bf16) for i in range(2)]
        ks = [sb(f"ks{i}", [ROWS_DIAG, 2, HG, HALF], bf16) for i in range(2)]
        vs = [sb(f"vs{i}", [P, BT, HG, 32]) for i in range(2)]
        ot = [sb(f"ot{i}", [P, HALF]) for i in range(2)]
        causal_sb = sb("causal_sb", [P, HALF])
        junk = [sb(f"junk{i}", [P, HALF], bf16) for i in range(2)]
        ident = sb("ident", [P, P])
        before_sb = sb("before_sb", [P, P], bf16)
        ones_bf = sb("ones_bf", [P, P], bf16)
        wq_sb, wk_sb, wv_sb, wo_sb = [sb(n, [P, C]) for n in ("wq_sb", "wk_sb", "wv_sb", "wo_sb")]
        wr_sb = sb("wr_sb", [P, E])
        bias_qk = sb("bias_qk", [P, 2])
        bias_q_scaled = sb("bias_q_scaled", [P, 1])
        bv_row = sb("bv_row", [P, C])
        bo_row = sb("bo_row", [P, C])
        stat = sb("stat", [P, 5, BT])
        mx = sb("mx", [P, 2, HG * QT])
        mx_late = sb("mx_late", [P, HG * QT])
        mx_all = sb("mx_all", [P, HG * QT])
        mt = [sb(f"mt{i}", [HG * QT, PARTS, P], bf16) for i in range(2)]
        mrest = sb("mrest", [HG * QT, P])
        rden = sb("rden", [P, 2, HG * QT])
        logits = sb("logits", [P, NT * E])
        rt = [sb(f"rt{i}", [P, NT * E]) for i in range(6)]
        mask_bf = sb("mask_bf", [P, NT * E], bf16)
        rs = sb("rs", [P, 5, NT])
        ex = sb("ex", [P, 6, E])
        exi = sb("exi", [P, 2, E], i32)
        eidx = sb("eidx", [P, NT * E])
        meta = sb("meta", [P, NT, TOPK, 3])
        tile_no = sb("tile_no", [1, SLOT_TILES])
        owner = sb("owner", [1, SLOT_TILES * E])
        owner_f = sb("owner_f", [1, SLOT_TILES])
        owner_i = sb("owner_i", [1, SLOT_TILES], i32)
        stage = [sb(f"stage{i}", [P, ROW]) for i in range(2)]
        stage_idx = [sb(f"stage_idx{i}", [P, 1], u32) for i in range(2)]
        padrow = sb("padrow", [P, PAD, ROW])
        row_in = [sb(f"row_in{i}", [P, ROW]) for i in range(4)]
        row_t = [sb(f"row_t{i}", [P, P]) for i in range(2)]
        gate = [sb(f"gate{i}", [P, HID]) for i in range(2)]
        hid = [sb(f"hid{i}", [P, HID]) for i in range(2)]
        wgu = [sb(f"wgu{i}", [P, 2 * HID]) for i in range(2)]
        y_out = [sb(f"y_out{i}", [P, C]) for i in range(2)]
        y_idx = [sb(f"y_idx{i}", [P, 1], u32) for i in range(4)]
        heads = ot
        xres = vall
        at_sb = [prob_sb[:, i * HALF:(i + 1) * HALF] for i in range(2)]
        yres = [prob_sb[:, i * 2 * HALF:(i + 1) * 2 * HALF] for i in range(2)]
        fin = [prob_sb[:, (4 + i) * HALF:(5 + i) * HALF] for i in range(2)]

        s_const, s_bias, s_fixed, s_ones, s_pad, s_padded, s_iota = [sem("s_" + n) for n in (
            "const", "bias", "fixed", "ones", "pad", "padded", "iota")]
        s_x, s_rest, s_part2, s_part3, s_split = [sems("s_" + n) for n in ("x", "rest", "part2", "part3", "split")]
        s_xc, s_sq, s_var, s_std, s_ln, s_xn, s_xt_ps, s_xt, s_qk_ps, s_qk, s_v_ps, s_v, s_lg_ps, s_lg = [
            sem("s_" + n) for n in ("xc", "sq", "var", "std", "ln", "xn", "xt_ps", "xt", "qk_ps", "qk", "v_ps", "v",
                                    "lg_ps", "lg")]
        s_rt, s_gap, s_gap_exp, s_mask, s_count, s_meta, s_owner, s_weights = [sem("s_" + n) for n in (
            "rt", "gap", "gap_exp", "mask", "count", "meta", "owner", "weights")]
        s_load = [sems(f"s_load{i}_") for i in range(2)]
        s_chunk = sem("s_chunk")
        s_read = sem("s_read")
        s_mx = sem("s_mx")
        s_mpart = sem("s_mpart")
        s_mt = sem("s_mt")
        s_mrow = sems("s_mrow")
        s_score = sem("s_score")
        s_exp = sem("s_exp")
        s_causal = sem("s_causal")
        s_vcopy = sem("s_vcopy")
        s_pv = sem("s_pv")
        s_ocopy = sem("s_ocopy")
        s_ot = sem("s_ot")
        s_rden = sem("s_rden")
        s_norm = sem("s_norm")
        s_staged = sem("s_staged")
        s_scatter = sems("s_scatter")
        s_xres, s_xbo, s_heads, s_at_ps, s_at, s_wo, s_res = [sem("s_" + n) for n in (
            "xres", "xbo", "heads", "at_ps", "at", "wo", "res")]
        s_row = sems("s_row", 4)
        s_row_ps, s_row_t, s_wgu, s_gate_ps, s_up_ps, s_gate, s_hid, s_y_ps, s_y, s_yidx = [
            sem("s_" + n) for n in ("row_ps", "row_t", "wgu", "gate_ps", "up_ps", "gate", "hid", "y_ps", "y", "yidx")]
        s_routed = sems("s_routed")
        s_yres = sems("s_yres")
        s_acc, s_fin = sem("s_acc"), sem("s_fin")
        s_out = sems("s_out")

        block = ctx.enter_context(nc.Block())
        CONST = 12 * 16
        GROUP_LOAD = 7 * 16

        def wait_apart(eng, waited, count):
            eng.wait_ge(waited, count.v())
            if count.i is not None:
                eng.nop(nofuse=True)

        def loop_of_groups(eng, step, last):
            with eng.Fori(0, last // 2) as i:
                for k in range(2):
                    step(Count(1 + k, i, 2))

        def loop_of_slots(eng, step):
            for s in range(4):
                step(Count(s))
            with eng.Fori(0, SLOT_TILES // 4 - 2) as i:
                for k in range(4):
                    step(Count(4 + k, i, 4))
            for s in range(SLOT_TILES - 4, SLOT_TILES):
                step(Count(s))

        def turn0(g):
            return g * SEQ + SEQ0

        def chunk_turn(u, h):
            return HG * u + h + (u >= 1) + (u >= 5)

        def first_turn(u, h):
            return HG * u + h + (u >= 5)

        MT1_TURN, MT0_TURN = HG, 5 * HG + 1

        @block.sync
        def _(sp):
            for b in range(2):
                sp.dma_start(xb[b].rearrange("p (j c) -> p j c", c=C),
                             x[b].rearrange("(j p) c -> p j c", p=P)).then_inc(s_x[b], 16)
            for dst, src in ((ident[:, :], eye), (wq_sb[:, :], Wq), (wk_sb[:, :], Wk), (wv_sb[:, :], Wv),
                             (wo_sb[:, :], Wo), (wr_sb[:, :], Wr), (before_sb[:, :].bitcast(u16), before),
                             (causal_sb[:, :], causal),
                             (bias_qk[:, 0:1], bq.rearrange("(c a) -> c a", a=1)),
                             (bias_qk[:, 1:2], bk.rearrange("(c a) -> c a", a=1)),
                             (bv_row[:, :], bv.rearrange("(a c) -> a c", a=1).to_broadcast([P, C])),
                             (bo_row[:, :], bo.rearrange("(a c) -> a c", a=1).to_broadcast([P, C]))):
                sp.dma_start(dst, src).then_inc(s_const, 16)

            def next_tokens(b):
                sp.wait_ge(s_xc, b - 1)
                sp.dma_start(xb[b % 2].rearrange("p (j c) -> p j c", c=C),
                             x[b].rearrange("(j p) c -> p j c", p=P)).then_inc(s_x[b % 2], 16)

            for stacks, fixed in ((qs, fixed_q), (ks, fixed_k)):
                for par in range(2):
                    sp.dma_start(stacks[par][ROW_ONE:ROWS_DIAG, :, :, :].rearrange("r f h t -> r (f h t)")
                                 .rearrange("r (m t) -> r m t", t=P).bitcast(u16),
                                 fixed.unsqueeze(1).to_broadcast([ROWS_DIAG - ROW_ONE, 2 * HG * QT, P])
                                 ).then_inc(s_fixed, 16)

            def load(g, hf):
                par = g % 2
                gi = g.v()
                lo = hf * HALF
                done = s_load[par][hf]
                for i in range(PARTS):
                    rows = slice(i * PARTS * HD, (i + 1) * PARTS * HD)
                    sp.dma_start(qs[par][rows, hf, :, :],
                                 q_split[bass.ds(gi, 1), :, i * HD:(i + PARTS) * HD, lo:lo + HALF]
                                 .rearrange("g h r t -> r (g h) t")).then_inc(done, 16)
                    sp.dma_start(ks[par][rows, hf, :, :],
                                 k_split[bass.ds(gi, 1), :, :, lo:lo + HALF]
                                 .rearrange("g h r t -> r (g h) t")).then_inc(done, 16)
                sp.dma_start(ks[par][ROW_ONE:ROW_ZERO, hf, :, :].bitcast(u16),
                             alibi[bass.ds(gi, 1), :, :, lo:lo + HALF]
                             .rearrange("g i h t -> i (g h) t")).then_inc(done, 16)

            for b in range(B):
                if b + 2 < B:
                    next_tokens(b + 2)
                for s, dst in enumerate((q_split, k_split)):
                    sp.wait_ge(s_part3[s], b + 1)
                    mine = dst[b * NHG:(b + 1) * NHG].rearrange("g h r t -> (g h) r t")
                    for k in range(2 * PARTS - 1 if s == 0 else PARTS):
                        sp.dma_start(mine[:, k * HD:(k + 1) * HD, :],
                                     split[b % 2][:, s, k % PARTS, :]).then_inc(s_split[b % 2], 16)
                if b == 1:
                    sp.wait_ge(s_split[0], 8 * 16)
                    sp.wait_ge(s_fixed, 4 * 16)
                    for g in range(2):
                        for hf in range(2):
                            load(Count(g), hf)
            for i in range(2):
                sp.wait_ge(s_split[i], 8 * 16 * (B // 2))

            def place_maxima(g, hf):
                sp.wait_ge(s_mt, (g * 2 + (hf + 1)).v())
                for i in range(PARTS):
                    dst = qs[g % 2][ROW_MAX + i:ROW_MAX + i + 1, hf, :, :].rearrange("p h t -> p (h t)")
                    sp.dma_start(dst.rearrange("p (m t) -> p m t", t=P), mt[hf][:, i, :]).then_inc(s_mrow[hf], 16)

            place_maxima(Count(0), 0)

            def expert_weights(g):
                e = (g + -1).v()
                at = e * HID
                sp.dma_start(wg_sb[:, bass.ds(at, HID)],
                             Wg[bass.ds(e, 1)].rearrange("e c h -> c (e h)")).then_inc(s_weights, 16)
                sp.dma_start(wu_sb[:, bass.ds(at, HID)],
                             Wu[bass.ds(e, 1)].rearrange("e c h -> c (e h)")).then_inc(s_weights, 16)
                sp.dma_start(wd_sb[:, bass.ds(at, HID)].rearrange("p (j c) -> p j c", c=C),
                             Wd[bass.ds(e, 1)].rearrange("e (j p) c -> p (e j) c", p=P)).then_inc(s_weights, 16)

            def step(g, loads=True, maxima=True, weights=False):
                place_maxima(g, 1)
                if maxima:
                    place_maxima(g + 1, 0)
                if weights:
                    expert_weights(g)
                if loads:
                    sp.wait_ge(s_score, (g * 24 + 16).v())
                    load(g + 2, 0)
                    sp.wait_ge(s_score, (g * 24 + 24).v())
                    load(g + 2, 1)

            step(Count(0))
            sp.wait_ge(s_lg_ps, B)
            with sp.Fori(0, E // 2) as i:
                for k in range(2):
                    step(Count(1 + k, i, 2), weights=True)
            with sp.Fori(E // 2, (G - 4) // 2) as i:
                for k in range(2):
                    step(Count(1 + k, i, 2))
            step(Count(G - 3))
            step(Count(G - 2), loads=False)
            step(Count(G - 1), loads=False, maxima=False)

            sp.wait_ge(s_vcopy, G)
            for b in range(B):
                sp.dma_start(xres[:, b * T:(b + 1) * T].rearrange("p (j c) -> p j c", c=C),
                             x[b].rearrange("(j p) c -> p j c", p=P)).then_inc(s_xres, 16)

            sp.wait_ge(s_padded, 16 * (SLOT_TILES // PAD))
            for r in range(TOPK):
                sp.wait_ge(s_scatter[r], 16 * NT)

            def rows(s):
                if s.a or s.c >= 4:
                    sp.wait_ge(s_y, (s + -3).v())
                    sp.wait_ge(s_yidx, (s + -3).v())
                at = s.v() * P if s.a == 0 else s.i * (s.a * P) + s.c * P
                sp.dma_start(row_in[s % 4][:, :], slots[bass.ds(at, P), :]).then_inc(s_row[s % 4], 16)

            for s in range(4):
                rows(Count(s))
            with sp.Fori(1, SLOT_TILES // 4) as i:
                for k in range(4):
                    rows(Count(k, i, 4))

            for r in range(TOPK):
                sp.wait_ge(s_routed[r], 16 * (SLOT_TILES // 2))
            for n in range(NT // QT):
                if n >= 2:
                    sp.wait_ge(s_fin, n - 1)
                sp.dma_start(yres[n % 2].rearrange("p (j c) -> p j c", c=TOPK * C),
                             routed[n * QT * P * TOPK:(n + 1) * QT * P * TOPK, :]
                             .rearrange("(j p r) c -> p j (r c)", p=P, r=TOPK)).then_inc(s_yres[n % 2], 16)

        @block.gpsimd
        def _(pool):
            nc.gpsimd.memset(padrow[:, :, :], 0.0).then_inc(s_pad, 1)
            pool.wait_ge(s_pad, 1)
            nc.gpsimd.iota(padrow[:, :, C + 1], pattern=[[P, PAD]], base=N * TOPK, channel_multiplier=1,
                           allow_small_or_imprecise_dtypes=True).then_inc(s_pad, 1)
            nc.gpsimd.memset(ones_bf[:, :], 1.0).then_inc(s_ones, 1)
            for i in range(2):
                nc.gpsimd.memset(vs[i][:, :, :, :], 0.0).then_inc(s_ones, 1)
            pool.wait_ge(s_ones, 3)
            for i in range(2):
                nc.gpsimd.memset(vs[i][:, :, :, HD:HD + 1], 1.0).then_inc(s_ones, 1)
            nc.gpsimd.iota(eidx[:, :], pattern=[[0, NT], [1, E]], base=0, channel_multiplier=0,
                           allow_small_or_imprecise_dtypes=True).then_inc(s_iota, 1)
            nc.gpsimd.iota(tile_no[:, :], pattern=[[1, SLOT_TILES]], base=0, channel_multiplier=0,
                           allow_small_or_imprecise_dtypes=True).then_inc(s_iota, 1)
            nc.gpsimd.iota(meta[:, :, :, 1], pattern=[[TOPK * P, NT], [1, TOPK]], base=0, channel_multiplier=TOPK,
                           allow_small_or_imprecise_dtypes=True).then_inc(s_iota, 1)
            for b in range(B):
                parts = split[b % 2][:, 1]
                pool.wait_ge(s_qk, 4 * b + 4)
                if b:
                    pool.wait_ge(s_part3[1], b)
                nc.gpsimd.tensor_tensor(rest[1], full[1], parts[:, 0, :], ALU.subtract).then_inc(s_rest[1], 1)
                pool.wait_ge(s_rest[1], b + 1)
                nc.gpsimd.tensor_copy(parts[:, 1, :], rest[1]).then_inc(s_part2[1], 1)
                pool.wait_ge(s_part2[1], b + 1)
                nc.gpsimd.tensor_tensor(parts[:, 2, :], rest[1], parts[:, 1, :], ALU.subtract).then_inc(s_part3[1], 1)

            def copy_values(g):
                gi = g.v()
                at = gi * (BT * HG * HD)
                nc.gpsimd.tensor_copy(vs[g % 2][:, :, :, 0:HD].rearrange("p j c d -> p (j c) d"),
                                      vall[:, bass.ds(at, BT * HG * HD)].rearrange("p (m d) -> p m d", d=HD)
                                      ).then_inc(s_vcopy, 1)

            pool.wait_ge(s_v, 2 * B)
            copy_values(Count(0))
            pool.wait_ge(s_meta, 1)
            pool.wait_ge(s_padded, 16 * (SLOT_TILES // PAD))

            def scatter(g, k, r):
                n = g * 2 + k
                gi = g.v()
                if g.a or n.c >= 1:
                    wait_apart(pool, s_scatter[r], n * 16)
                nc.gpsimd.tensor_copy(stage[r][:, 0:C], xn[:, bass.ds(gi * (2 * C) + k * C, C)]).then_inc(s_staged, 1)
                mine = meta[:, bass.ds(gi * 2 + k, 1), r, :].rearrange("p a m -> p (a m)")
                nc.gpsimd.tensor_copy(stage[r][:, C:ROW], mine[:, 0:2]).then_inc(s_staged, 1)
                nc.gpsimd.tensor_copy(stage_idx[r][:, :], mine[:, 2:3]).then_inc(s_staged, 1)
                wait_apart(pool, s_staged, n * 6 + (3 * r + 3))
                pool.indirect_dma_start(slots[:, :], bass.IndirectOffsetOnAxis(ap=stage_idx[r][:, :], axis=0),
                                        stage[r][:, :], None).then_inc(s_scatter[r], 16)

            def step(g, values=True):
                if values:
                    if g.a or g.c:
                        wait_apart(pool, s_pv, g * UNITS)
                    copy_values(g + 1)
                diagonal = 0
                for u in range(UNITS):
                    if prob_unit(u)[3]:
                        diagonal += 1
                        wait_apart(pool, s_exp, g * 24 + (2 * u + 2))
                        first = prob[u % 2][:, :, 0:P]
                        nc.gpsimd.affine_select(out=first, in_=first, compare_op=ALU.is_ge, fill=0.0, base=0,
                                                pattern=[[0, HG], [1, P]], channel_multiplier=-1).then_inc(s_causal, 1)
                    elif u == 4:
                        for k in range(2):
                            for r in range(TOPK):
                                scatter(g, k, r)

            step(Count(0))
            loop_of_groups(pool, step, G - 2)
            step(Count(G - 1), values=False)

            def put(s):
                pool.wait_ge(s_yidx, (s + 1).v())
                wait_apart(pool, s_y, s + 1)
                pool.indirect_dma_start(routed[:, :], bass.IndirectOffsetOnAxis(ap=y_idx[s % 4][:, :], axis=0),
                                        y_out[s % 2][:, :], None).then_inc(s_routed[s % 2], 16)

            loop_of_slots(pool, put)

        @block.scalar
        def _(act):
            act.wait_ge(s_const, CONST)
            nc.scalar.mul(bias_q_scaled[:, :], bias_qk[:, 0:1], HD ** -0.5).then_inc(s_bias, 1)
            act.wait_ge(s_bias, 1)

            def norm(b):
                act.wait_ge(s_xc, b + 1)
                if b:
                    act.wait_ge(s_var, b)
                nc.scalar.activation(sq, xn[:, b * T:(b + 1) * T], ACT.Square).then_inc(s_sq, 1)
                act.wait_ge(s_var, b + 1)
                if b:
                    act.wait_ge(s_xn, b)
                nc.scalar.activation(stat[:, 2, :], stat[:, 1, :], ACT.Sqrt).then_inc(s_std, 1)

            norm(0)
            for b in range(B):
                for i in range(2):
                    act.wait_ge(s_xt_ps, 2 * b + i + 1)
                    if b >= 2 and i == 0:
                        act.wait_ge(s_lg_ps, b - 1)
                    nc.scalar.copy(xt[b % 2][:, i * HALF:(i + 1) * HALF], ps[:, i, :]).then_inc(s_xt, 1)
                if b + 1 < B:
                    norm(b + 1)
                for s in range(2):
                    act.wait_ge(s_qk_ps, 2 * b + s + 1)
                    if b:
                        act.wait_ge(s_part2[s], b)
                    if b >= 2:
                        act.wait_ge(s_split[b % 2], 8 * 16 * (b // 2))
                    src = ps[:, 2 + 2 * s:4 + 2 * s, :].rearrange("p a t -> p (a t)")
                    bias, scale = (bias_q_scaled[:, :], HD ** -0.5) if s == 0 else (bias_qk[:, 1:2], 1.0)
                    for dst in (full[s], split[b % 2][:, s, 0, :]):
                        nc.scalar.activation(dst, src, ACT.Identity, bias=bias, scale=scale).then_inc(s_qk, 1)

            act.wait_ge(s_gap, 1)
            nc.scalar.activation(rs[:, 4, :], rs[:, 3, :], ACT.Exp).then_inc(s_gap_exp, 1)
            act.wait_ge(s_split[1], 8 * 16 * (B // 2))
            act.wait_ge(s_pad, 2)
            for i in range(SLOT_TILES // PAD):
                act.dma_start(slots[i * PAD * P:(i + 1) * PAD * P, :].rearrange("(j p) c -> p j c", p=P),
                             padrow[:, :, :]).then_inc(s_padded, 16)


            def take_out(g, hf):
                act.wait_ge(s_pv, (g * UNITS + (4 if hf == 0 else UNITS)).v())
                nc.scalar.copy(ot[hf][:, :], ps[:, 6 + hf, :]).then_inc(s_ocopy, 1)

            def step(g):
                for u in range(UNITS):
                    q0 = prob_unit(u)[2]
                    n = HALF - q0
                    if g.a or g.c or u >= 2:
                        act.wait_ge(s_pv, (g * UNITS + (u - 1)).v())
                    for pair in range(2):
                        act.wait_ge(s_score, (g * 24 + (2 * u + pair + 1)).v())
                        nc.scalar.activation(prob[u % 2][:, 2 * pair:2 * pair + 2, 0:n],
                                             ps[:, 2 * pair:2 * pair + 2, 0:n], ACT.Exp).then_inc(s_exp, 1)
                    if u == 0 and (g.a or g.c):
                        take_out(g + -1, 1)
                    if u == 4:
                        take_out(g, 0)

            step(Count(0))
            loop_of_groups(act, step, G - 2)
            step(Count(G - 1))
            take_out(Count(G - 1), 1)

            def copy_row(s):
                act.wait_ge(s_row_ps, (s + 1).v())
                nc.scalar.copy(row_t[s % 2][:, :], ps[:, 4 + s % 2, 0:P]).then_inc(s_row_t, 1)

            copy_row(Count(0))
            copy_row(Count(1))

            act.wait_ge(s_pv, UNITS * G)
            for n in range(NT // QT):
                act.wait_ge(s_at_ps, n + 1)
                if n >= 2:
                    act.wait_ge(s_wo, n - 1)
                nc.scalar.copy(at_sb[n % 2][:, :], ps[:, n % 2, :]).then_inc(s_at, 1)

            def silu(s):
                act.wait_ge(s_gate_ps, (s + 1).v())
                if s.a or s.c >= 2:
                    act.wait_ge(s_hid, (s + -1).v())
                nc.scalar.activation(gate[s % 2][:, :], ps[:, s % 2, :], ACT.Silu).then_inc(s_gate, 1)

            def weigh(s):
                act.wait_ge(s_y_ps, (s + 1).v())
                if s.a or s.c >= 2:
                    act.wait_ge(s_routed[s % 2], (s // 2 * 16).v())
                nc.scalar.activation(y_out[s % 2][:, :], ps[:, 6 + s % 2, 0:C], ACT.Copy,
                                     scale=row_in[s % 4][:, C:C + 1]).then_inc(s_y, 1)

            act.wait_ge(s_res, NT // QT)
            silu(Count(0))

            def expert(s):
                peeled = not s.a
                if not peeled or s.c + 1 < SLOT_TILES:
                    silu(s + 1)
                if not peeled or s.c + 2 < SLOT_TILES:
                    copy_row(s + 2)
                weigh(s)

            loop_of_slots(act, expert)
            for n in range(NT // QT):
                act.wait_ge(s_fin, n + 1)
                b, hf = divmod(n, 2)
                act.dma_start(out[b, hf * HALF:(hf + 1) * HALF].rearrange("(j p) c -> p j c", p=P),
                              fin[n % 2].rearrange("p (j c) -> p j c", c=C)).then_inc(s_out[n % 2], 16)
            for i in range(2):
                act.wait_ge(s_out[i], 16 * (NT // QT // 2))

        @block.vector
        def _(dve):
            chain = [0]

            def link(ins):
                chain[0] += 1
                ins.then_inc(s_ln, 1)
                dve.wait_ge(s_ln, chain[0])

            inv, var, std, r, t = [stat[:, i, :] for i in range(5)]

            def col(a):
                return a.unsqueeze(2).to_broadcast([P, BT, C])

            def tiles(a):
                return a.rearrange("p (j c) -> p j c", c=C)

            def norm(b):
                dve.wait_ge(s_x[b % 2], 16 * (b // 2 + 1))
                link(nc.vector.tensor_reduce(inv, tiles(xb[b % 2]), AX.X, ALU.add))
                link(nc.vector.tensor_scalar(t, inv, 1.0 / C, None, ALU.mult))
                mine = tiles(xn[:, b * T:(b + 1) * T])
                nc.vector.tensor_tensor(mine, tiles(xb[b % 2]), col(t), ALU.subtract).then_inc(s_xc, 1)
                dve.wait_ge(s_sq, b + 1)
                link(nc.vector.tensor_reduce(inv, tiles(sq), AX.X, ALU.add))
                nc.vector.tensor_scalar(var, inv, 1.0 / C, EPS, ALU.mult, ALU.add).then_inc(s_var, 1)
                dve.wait_ge(s_var, b + 1)
                dve.wait_ge(s_std, b + 1)
                link(nc.vector.reciprocal(r, std))
                link(nc.vector.tensor_tensor(t, r, r, ALU.mult))
                link(nc.vector.tensor_tensor(t, t, var, ALU.mult))
                link(nc.vector.tensor_scalar(t, t, -0.5, 1.5, ALU.mult, ALU.add))
                link(nc.vector.tensor_tensor(t, t, r, ALU.mult))
                nc.vector.tensor_tensor(mine, mine, col(t), ALU.mult).then_inc(s_xn, 1)

            def split_queries(b):
                parts = split[b % 2][:, 0]
                dve.wait_ge(s_qk, 4 * b + 2)
                nc.vector.tensor_tensor(rest[0], full[0], parts[:, 0, :], ALU.subtract).then_inc(s_rest[0], 1)
                dve.wait_ge(s_rest[0], b + 1)
                nc.vector.tensor_copy(parts[:, 1, :], rest[0]).then_inc(s_part2[0], 1)
                dve.wait_ge(s_part2[0], b + 1)
                nc.vector.tensor_tensor(parts[:, 2, :], rest[0], parts[:, 1, :], ALU.subtract).then_inc(s_part3[0], 1)

            def values(b):
                dve.wait_ge(s_v_ps, b + 1)
                dst = vall[:, b * T:(b + 1) * T].rearrange("p (g j c) -> p j g c", g=NHG, j=BT)
                for i in range(2):
                    for j in range(4):
                        last = nc.vector.tensor_tensor(
                            dst[:, 4 * i + j],
                            ps[:, 6 + i, j * P:(j + 1) * P].rearrange("p (g c) -> p g c", g=NHG),
                            bv_row[:, :].rearrange("p (g c) -> p g c", g=NHG), ALU.add)
                    last.then_inc(s_v, 1)
                dve.wait_ge(s_lg_ps, b + 1)
                nc.vector.tensor_copy(logits[:, b * BT * E:(b + 1) * BT * E], ps[:, 0, 0:BT * E]).then_inc(s_lg, 1)

            norm(0)
            dve.wait_ge(s_const, CONST)
            for b in range(B):
                if b + 1 < B:
                    norm(b + 1)
                split_queries(b)
                values(b)

            def by_token(a):
                return a.rearrange("p (n e) -> p n e", e=E)

            def over_e(a):
                return a.unsqueeze(2).to_broadcast([P, NT, E])

            hit, pick1, pick2, masked, work, pos = [by_token(a[:, :]) for a in rt]
            lg, ei = by_token(logits[:, :]), by_token(eidx[:, :])
            v1, v2, idx, gap, egap = [rs[:, i, :] for i in range(5)]
            dve.wait_ge(s_lg, B)
            dve.wait_ge(s_iota, 3)

            def top(values, best, pick):
                link(nc.vector.tensor_reduce(best, values, AX.X, ALU.max))
                link(nc.vector.tensor_tensor(hit, values, over_e(best), ALU.is_equal))
                link(nc.vector.scalar_tensor_tensor(work, hit, -float(E), ei, ALU.mult, ALU.add))
                link(nc.vector.tensor_reduce(idx, work, AX.X, ALU.min))
                link(nc.vector.tensor_scalar(idx, idx, float(E), None, ALU.add))
                link(nc.vector.tensor_tensor(pick, ei, over_e(idx), ALU.is_equal))

            top(lg, v1, pick1)
            link(nc.vector.scalar_tensor_tensor(masked, pick1, NEG, lg, ALU.mult, ALU.add))
            top(masked, v2, pick2)
            nc.vector.tensor_tensor(gap, v2, v1, ALU.subtract).then_inc(s_gap, 1)
            nc.vector.tensor_tensor(by_token(mask_bf[:, :]), pick1, pick2, ALU.add).then_inc(s_mask, 1)
            dve.wait_ge(s_gap_exp, 1)
            link(nc.vector.tensor_scalar(v1, egap, 1.0, None, ALU.add))
            link(nc.vector.reciprocal(v2, v1))
            link(nc.vector.tensor_scalar(v2, v2, float(DEPTH_SCALE), None, ALU.mult))
            nc.vector.tensor_copy(meta[:, :, 0, 0], v2)
            link(nc.vector.tensor_tensor(meta[:, :, 1, 0], v2, egap, ALU.mult))
            dve.wait_ge(s_count, 1)
            counts, upto, start = rt[3][:, :], rt[4][:, :], rt[0][:, :]
            ones_row = rt[5][:, :]
            link(nc.vector.memset(ones_row, 1.0))
            link(nc.vector.tensor_copy(counts.rearrange("p (e n) -> p e n", e=E),
                                       ps[:, 1, 0:NT * E].rearrange("p (n e) -> p e n", e=E)))
            link(nc.vector.tensor_tensor_scan(upto, ones_row, counts, 0.0, ALU.mult, ALU.add))
            link(nc.vector.tensor_tensor(start, upto, counts, ALU.subtract))
            by_e = [a.rearrange("p (e n) -> p e n", e=E) for a in (upto, start)]
            link(nc.vector.tensor_tensor(ex[:, 0, :], by_e[0][:, :, NT - 1], by_e[1][:, :, 0], ALU.subtract))
            link(nc.vector.tensor_scalar(exi[:, 0, :], ex[:, 0, :], float(P - 1), None, ALU.add))
            link(nc.vector.tensor_scalar(exi[:, 1, :], exi[:, 0, :], int(np.log2(P)), None, ALU.logical_shift_right))
            link(nc.vector.tensor_copy(ex[:, 1, :], exi[:, 1, :]))
            link(nc.vector.tensor_tensor_scan(ex[:, 2, :], ones_row[:, 0:E], ex[:, 1, :], 0.0, ALU.mult, ALU.add))
            link(nc.vector.tensor_tensor(ex[:, 3, :], ex[:, 2, :], ex[:, 1, :], ALU.subtract))
            link(nc.vector.scalar_tensor_tensor(ex[:, 4, :], ex[:, 3, :], float(P), by_e[1][:, :, 0],
                                                ALU.mult, ALU.subtract))
            link(nc.vector.tensor_tensor(by_token(counts), by_e[1].rearrange("p e n -> p n e"),
                                         by_token(ps[:, 0, 0:NT * E]), ALU.add))
            link(nc.vector.tensor_tensor(pos, by_token(counts),
                                         ex[:, 4, :].unsqueeze(1).to_broadcast([P, NT, E]), ALU.add))
            for k, pick in enumerate((pick1, pick2)):
                link(nc.vector.tensor_tensor(work, pick, pos, ALU.mult))
                last = nc.vector.tensor_reduce(meta[:, :, k, 2], work, AX.X, ALU.add)
                if k == 0:
                    link(last)
            last.then_inc(s_meta, 1)
            own = owner[:, :].rearrange("p (n e) -> p n e", e=E)
            link(nc.vector.tensor_tensor(own, ex[0:1, 2, :].unsqueeze(1).to_broadcast([1, SLOT_TILES, E]),
                                         tile_no[:, :].unsqueeze(2).to_broadcast([1, SLOT_TILES, E]), ALU.is_le))
            link(nc.vector.tensor_reduce(owner_f[:, :], own, AX.X, ALU.add))
            nc.vector.tensor_scalar(owner_i[:, :], owner_f[:, :], float(E - 1), None, ALU.min).then_inc(s_owner, 1)

            def read_chunk(g, turn, u, h):
                qt, kh, n, diagonal = max_unit(u)
                dst = mx_late[:, :] if kh else mx[:, qt // QT, :]
                dst = dst[:, h * QT + qt % QT:h * QT + qt % QT + 1]
                src = ps[:, 4 + turn % 2, 0:n]
                if diagonal:
                    wait_apart(dve, s_chunk, turn + 1)
                else:
                    dve.wait_ge(s_chunk, (turn + 1).v())
                if diagonal:
                    ins = nc.vector.tensor_tensor_reduce(out=junk[turn % 2][:, 0:n], in0=src, in1=causal_sb[:, HALF - n:HALF],
                                                         scale=1.0, scalar=NEG, op0=ALU.add, op1=ALU.max,
                                                         accum_out=dst)
                else:
                    ins = nc.vector.tensor_reduce(dst, src, AX.X, ALU.max)
                ins.then_inc(s_read, 1)

            def join_maxima(g, turn):
                dve.wait_ge(s_read, turn.v())
                nc.vector.tensor_tensor(mx_all[:, :], mx[:, 1, :], mx_late[:, :], ALU.max).then_inc(s_mx, 1)

            def split_maxima(g, hf, turn):
                event = g * 2 + hf
                dve.wait_ge(s_chunk, (turn + 1).v())
                if g.a or g.c:
                    dve.wait_ge(s_mrow[hf], (g * (PARTS * 16)).v())
                src = ps[0:HG * QT, 4 + turn % 2, 0:P]
                dst = mt[hf]
                nc.vector.tensor_scalar(dst[:, 0, :], src, -1.0, None, ALU.mult).then_inc(s_mpart, 1)
                dve.wait_ge(s_mpart, (event * 2 + 1).v())
                nc.vector.scalar_tensor_tensor(mrest[:, :], src, -1.0, dst[:, 0, :], ALU.mult,
                                               ALU.subtract).then_inc(s_read, 1)
                dve.wait_ge(s_read, (turn + 1).v())
                nc.vector.tensor_copy(dst[:, 1, :], mrest[:, :]).then_inc(s_mpart, 1)
                dve.wait_ge(s_mpart, (event * 2 + 2).v())
                nc.vector.tensor_tensor(dst[:, 2, :], mrest[:, :], dst[:, 1, :], ALU.subtract).then_inc(s_mt, 1)

            def divide(g, hf):
                dve.wait_ge(s_ot, (g * 2 + (hf + 1)).v())
                src = ps[:, 6 + hf, :].rearrange("p (m w) -> p m w", w=32)
                nc.vector.reciprocal(rden[:, hf, :], src[:, :, HD]).then_inc(s_rden, 1)
                dve.wait_ge(s_rden, (g * 2 + (hf + 1)).v())
                at = g.v() * (BT * HG * HD) + hf * P
                nc.vector.tensor_tensor(attn[:, bass.ds(at, P)].rearrange("p (m d) -> p m d", d=HD),
                                        src[:, :, 0:HD],
                                        rden[:, hf, :].unsqueeze(2).to_broadcast([P, HG * QT, HD]),
                                        ALU.mult).then_inc(s_norm, 1)

            for u in range(UNITS):
                for h in range(HG):
                    read_chunk(Count(0), Count(first_turn(u, h)), u, h)
                if u == 4:
                    split_maxima(Count(0), 0, Count(5 * HG))
            join_maxima(Count(0), Count(UNITS * HG + 1))

            def step(g, ahead=True):
                turn = turn0(g)
                for u in range(UNITS):
                    if ahead:
                        for h in range(HG):
                            read_chunk(g + 1, turn + chunk_turn(u, h), u, h)
                    if u == 0:
                        split_maxima(g, 1, turn + (MT1_TURN if ahead else 0))
                    if u == 2 and (g.a or g.c):
                        divide(g + -1, 1)
                    if u == 4 and ahead:
                        split_maxima(g + 1, 0, turn + MT0_TURN)
                    if u == 6:
                        divide(g, 0)
                if ahead:
                    join_maxima(g + 1, turn + SEQ)

            def copy_weights(s):
                if s.a or s.c >= 2:
                    dve.wait_ge(s_up_ps, (s + -1).v())
                e = dve.value_load(owner_i[0:1, bass.ds(s.v(), 1)], min_val=0, max_val=E - 1)
                both = weights[:, 0:2 * E * HID].rearrange("p (w x) -> p w x", w=2)
                nc.vector.tensor_copy(wgu[s % 2].rearrange("p (w x) -> p w x", w=2),
                                      both[:, :, bass.ds(e * HID, HID)]).then_inc(s_wgu, 1)

            step(Count(0))
            loop_of_groups(dve, step, G - 2)
            step(Count(G - 1), ahead=False)
            dve.wait_ge(s_xres, B * 16)
            for b in range(B):
                nc.vector.tensor_tensor(tiles(xres[:, b * T:(b + 1) * T]), tiles(xres[:, b * T:(b + 1) * T]),
                                        bo_row[:, :].unsqueeze(1).to_broadcast([P, BT, C]), ALU.add).then_inc(s_xbo, 1)
            dve.wait_ge(s_weights, 3 * E * 16)
            dve.wait_ge(s_owner, 1)
            copy_weights(Count(0))
            copy_weights(Count(1))
            divide(Count(G - 1), 1)

            for r in range(TOPK):
                dve.wait_ge(s_scatter[r], 16 * NT)
            dve.wait_ge(s_norm, 2 * G)
            dve.wait_ge(s_xbo, B)

            def gather_heads(n):
                b, hf = divmod(n, 2)
                if n >= 2:
                    dve.wait_ge(s_at_ps, n - 1)
                src = attn[:, b * T:(b + 1) * T].rearrange("p (g j c) -> p j g c", g=NHG, j=BT)
                dst = heads[n % 2][:, :].rearrange("p (j g c) -> p j g c", j=QT, g=NHG)
                nc.vector.tensor_copy(dst, src[:, hf * QT:(hf + 1) * QT]).then_inc(s_heads, 1)

            gather_heads(0)
            gather_heads(1)
            for n in range(NT // QT):
                if n + 2 < NT // QT:
                    gather_heads(n + 2)
                dve.wait_ge(s_wo, n + 1)
                nc.vector.tensor_tensor(xn[:, n * HALF:(n + 1) * HALF], ps[:, 2 + n % 2, :],
                                        xres[:, n * HALF:(n + 1) * HALF], ALU.add).then_inc(s_res, 1)

            def multiply(s):
                dve.wait_ge(s_gate, (s + 1).v())
                dve.wait_ge(s_up_ps, (s + 1).v())
                if s.a or s.c >= 2:
                    dve.wait_ge(s_y_ps, (s + -1).v())
                nc.vector.tensor_tensor(hid[s % 2][:, :], ps[:, 2 + s % 2, :], gate[s % 2][:, :],
                                        ALU.mult).then_inc(s_hid, 1)

            def expert(s):
                peeled = not s.a
                multiply(s)
                if not peeled or s.c + 2 < SLOT_TILES:
                    copy_weights(s + 2)
                dve.wait_ge(s_row[s % 4], (s // 4 * 16 + 16).v())
                if not peeled or s.c >= 4:
                    dve.wait_ge(s_routed[s % 2], (s // 2 * 16 + -16).v())
                nc.vector.tensor_copy(y_idx[s % 4][:, :], row_in[s % 4][:, C + 1:C + 2]).then_inc(s_yidx, 1)

            loop_of_slots(dve, expert)

            for n in range(NT // QT):
                dve.wait_ge(s_yres[n % 2], 16 * (n // 2 + 1))
                y = yres[n % 2].rearrange("p (j r c) -> p j r c", r=TOPK, c=C)
                mine = tiles(xn[:, n * HALF:(n + 1) * HALF])
                nc.vector.tensor_tensor(mine, mine, y[:, :, 0, :], ALU.add).then_inc(s_acc, 1)
                dve.wait_ge(s_acc, n + 1)
                if n >= 2:
                    dve.wait_ge(s_out[n % 2], 16 * (n // 2))
                nc.vector.tensor_tensor(tiles(fin[n % 2]), mine, y[:, :, 1, :], ALU.add).then_inc(s_fin, 1)

        @block.tensor
        def _(pe):
            pe.wait_ge(s_const, CONST)
            for b in range(B):
                pe.wait_ge(s_xn, b + 1)
                if b:
                    pe.wait_ge(s_xt, 2 * b)
                    pe.wait_ge(s_lg, b)
                for j in range(BT):
                    last = nc.tensor.transpose(ps[:, j // 4, (j % 4) * P:(j % 4 + 1) * P],
                                               xn[:, b * T + j * C:b * T + (j + 1) * C], ident[:, :])
                    if j % 4 == 3:
                        last.then_inc(s_xt_ps, 1)
                pe.wait_ge(s_xt, 2 * b + 2)
                for s, w in enumerate((wq_sb, wk_sb)):
                    if b:
                        pe.wait_ge(s_qk, 4 * (b - 1) + 2 * s + 2)
                    for i in range(2):
                        last = nc.tensor.matmul(ps[:, 2 + 2 * s + i, :], w[:, :],
                                                xt[b % 2][:, i * HALF:(i + 1) * HALF], start=True, stop=True)
                    last.then_inc(s_qk_ps, 1)
                if b:
                    pe.wait_ge(s_v, 2 * b)
                for j in range(BT):
                    last = nc.tensor.matmul(ps[:, 6 + j // 4, (j % 4) * P:(j % 4 + 1) * P],
                                            xt[b % 2][:, j * P:(j + 1) * P], wv_sb[:, :], start=True, stop=True)
                last.then_inc(s_v_ps, 1)
                for j in range(BT):
                    last = nc.tensor.matmul(ps[:, 0, j * E:(j + 1) * E], xt[b % 2][:, j * P:(j + 1) * P],
                                            wr_sb[:, :], start=True, stop=True)
                last.then_inc(s_lg_ps, 1)

            pe.wait_ge(s_mask, 1)
            pe.wait_ge(s_ones, 1)
            nc.tensor.matmul(ps[:, 0, 0:NT * E], before_sb[:, :], mask_bf[:, :], start=True, stop=True)
            nc.tensor.matmul(ps[:, 1, 0:NT * E], ones_bf[:, :], mask_bf[:, :], start=True, stop=True
                             ).then_inc(s_count, 1)

            def chunk(g, turn, u, h):
                qt, kh, n, _ = max_unit(u)
                if turn.a or turn.c >= 2:
                    pe.wait_ge(s_read, (turn + -1).v())
                nc.tensor.matmul(ps[:, 4 + turn % 2, 0:n],
                                 qs[g % 2][0:ROW_MAX, qt // QT, h, (qt % QT) * P:(qt % QT + 1) * P],
                                 ks[g % 2][0:ROW_MAX, kh, h, 0:n], start=True, stop=True).then_inc(s_chunk, 1)

            def wait_stacks(g, u):
                if u in (0, 4):
                    pe.wait_ge(s_load[g % 2][u // 4], (g // 2 * GROUP_LOAD + GROUP_LOAD).v())

            def transpose_maxima(src, turn):
                pe.wait_ge(s_read, (turn + -1).v())
                nc.tensor.transpose(ps[0:HG * QT, 4 + turn % 2, 0:P], src, ident[:, :]).then_inc(s_chunk, 1)

            def scores(g, u, pair):
                hf, kt, q0, diagonal = prob_unit(u)
                if pair == 0 and u in (0, 4):
                    pe.wait_ge(s_mrow[u // 4], (g * (PARTS * 16) + PARTS * 16).v())
                if g.a or g.c or u:
                    pe.wait_ge(s_exp, (g * 24 + (2 * u + pair - 1)).v())
                pieces = [(ROWS_DIAG, q0, q0 + P)] * diagonal + [(ROWS, q0 + P * diagonal, HALF)]
                for h in (2 * pair, 2 * pair + 1):
                    for rows, lo, hi in pieces:
                        if lo < hi:
                            last = nc.tensor.matmul(ps[:, h, lo - q0:hi - q0],
                                                    ks[g % 2][0:rows, kt // QT, h, (kt % QT) * P:(kt % QT + 1) * P],
                                                    qs[g % 2][0:rows, hf, h, lo:hi], start=True, stop=True)
                last.then_inc(s_score, 1)

            def products(g, u, piece):
                hf, kt, q0, diagonal = prob_unit(u)
                lo = q0 + piece * 2 * P
                hi = min(lo + 2 * P, HALF)
                if lo >= HALF:
                    return
                if piece == 0:
                    if diagonal:
                        pe.wait_ge(s_causal, (g * 8 + (u + 1 if u < 4 else u - 3)).v())
                    else:
                        pe.wait_ge(s_exp, (g * 24 + (2 * u + 2)).v())
                    if u == 0:
                        pe.wait_ge(s_vcopy, (g + 1).v())
                    if u in (0, 4) and (g.a or g.c):
                        pe.wait_ge(s_norm, (g * 2 + (-1 if u == 0 else 0)).v())
                for h in range(HG):
                    last = nc.tensor.matmul(ps[32 * h:32 * h + 32, 6 + hf, lo:hi], vs[g % 2][:, kt, h, :],
                                            prob[u % 2][:, h, lo - q0:hi - q0],
                                            start=(kt == 0 and piece == 0),
                                            stop=(kt == (QT - 1 if hf == 0 else BT - 1)))
                if hi == HALF:
                    last.then_inc(s_pv, 1)

            def transpose_result(g, hf):
                pe.wait_ge(s_ocopy, (g * 2 + (hf + 1)).v())
                for j in range(QT):
                    last = nc.tensor.transpose(ps[:, 6 + hf, j * P:(j + 1) * P], ot[hf][:, j * P:(j + 1) * P],
                                               ident[:, :])
                last.then_inc(s_ot, 1)

            pe.wait_ge(s_ones, 5)
            pe.wait_ge(s_fixed, 4 * 16)
            pe.wait_ge(s_qk, 4 * B)
            for u in range(UNITS):
                wait_stacks(Count(0), u)
                for h in range(HG):
                    chunk(Count(0), Count(first_turn(u, h)), u, h)
                if u == 4:
                    transpose_maxima(mx[:, 0, :], Count(5 * HG))
            pe.wait_ge(s_meta, 1)
            for pair in range(2):
                scores(Count(0), 0, pair)

            def step(g, ahead=True):
                turn = turn0(g)
                for u in range(UNITS):
                    if ahead:
                        wait_stacks(g + 1, u)
                    for pair in range(2):
                        if ahead:
                            chunk(g + 1, turn + chunk_turn(u, pair), u, pair)
                        if u + 1 < UNITS:
                            scores(g, u + 1, pair)
                        elif ahead:
                            scores(g + 1, 0, pair)
                    for piece in range(2):
                        if ahead:
                            chunk(g + 1, turn + chunk_turn(u, 2 + piece), u, 2 + piece)
                        products(g, u, piece)
                    if u == 0:
                        pe.wait_ge(s_mx, (g + 1).v())
                        transpose_maxima(mx_all[:, :], turn + (MT1_TURN if ahead else 0))
                    if u == 2 and (g.a or g.c):
                        transpose_result(g + -1, 1)
                    if u == 4 and ahead:
                        pe.wait_ge(s_read, (turn + (chunk_turn(3, HG - 1) + 1)).v())
                        transpose_maxima(mx[:, 0, :], turn + MT0_TURN)
                    if u == 6:
                        transpose_result(g, 0)

            step(Count(0))
            loop_of_groups(pe, step, G - 2)
            step(Count(G - 1), ahead=False)
            transpose_result(Count(G - 1), 1)

            def expert_of(s):
                return pe.value_load(owner_i[0:1, bass.ds(s.v(), 1)], min_val=0, max_val=E - 1)

            def transpose_row(s):
                pe.wait_ge(s_row[s % 4], (s // 4 * 16 + 16).v())
                if s.a or s.c >= 2:
                    pe.wait_ge(s_row_t, (s + -1).v())
                nc.tensor.transpose(ps[:, 4 + s % 2, 0:P], row_in[s % 4][:, 0:C], ident[:, :]).then_inc(s_row_ps, 1)

            pe.wait_ge(s_mt, 2 * G)
            transpose_row(Count(0))
            transpose_row(Count(1))

            def transpose_heads(n):
                if n >= 2:
                    pe.wait_ge(s_at, n - 1)
                pe.wait_ge(s_heads, n + 1)
                for j in range(QT):
                    last = nc.tensor.transpose(ps[:, n % 2, j * P:(j + 1) * P], heads[n % 2][:, j * P:(j + 1) * P],
                                               ident[:, :])
                last.then_inc(s_at_ps, 1)

            pe.wait_ge(s_exp, 24 * G)
            transpose_heads(0)
            for n in range(NT // QT):
                if n + 1 < NT // QT:
                    transpose_heads(n + 1)
                pe.wait_ge(s_at, n + 1)
                if n >= 2:
                    pe.wait_ge(s_res, n - 1)
                for j in range(QT):
                    last = nc.tensor.matmul(ps[:, 2 + n % 2, j * P:(j + 1) * P],
                                            at_sb[n % 2][:, j * P:(j + 1) * P], wo_sb[:, :], start=True, stop=True)
                last.then_inc(s_wo, 1)

            pe.wait_ge(s_owner, 1)
            pe.wait_ge(s_weights, 3 * E * 16)
            pe.wait_ge(s_res, NT // QT)

            def gate_up(s):
                pe.wait_ge(s_wgu, (s + 1).v())
                pe.wait_ge(s_row_t, (s + 1).v())
                if s.a or s.c >= 2:
                    pe.wait_ge(s_hid, (s + -1).v())
                for w, done in enumerate((s_gate_ps, s_up_ps)):
                    for j in range(HC):
                        at = w * HID + j * P
                        last = nc.tensor.matmul(ps[:, 2 * w + s % 2, j * P:(j + 1) * P], wgu[s % 2][:, at:at + P],
                                                row_t[s % 2][:, :], start=True, stop=True)
                    last.then_inc(done, 1)

            def down(s):
                e = expert_of(s)
                pe.wait_ge(s_hid, (s + 1).v())
                if s.a or s.c >= 2:
                    pe.wait_ge(s_y, (s + -1).v())
                for j in range(HC):
                    last = nc.tensor.matmul(ps[:, 6 + s % 2, 0:C], hid[s % 2][:, j * P:(j + 1) * P],
                                            wd_sb[:, bass.ds(e * HID + j * C, C)], start=(j == 0), stop=(j == HC - 1))
                last.then_inc(s_y_ps, 1)

            gate_up(Count(0))

            def expert(s):
                peeled = not s.a
                if not peeled or s.c + 1 < SLOT_TILES:
                    gate_up(s + 1)
                if not peeled or s.c + 2 < SLOT_TILES:
                    transpose_row(s + 2)
                down(s)

            loop_of_slots(pe, expert)


_INS = ['L0_attn_x', 'L0_attn_Wq', 'L0_attn_bq', 'L0_attn_Wk', 'L0_attn_bk', 'L0_attn_Wv', 'L0_attn_bv',
        'L0_attn_Wo', 'L0_attn_bo', 'L0_ffn_Wr', 'L0_ffn_Wg', 'L0_ffn_Wu', 'L0_ffn_Wd']


def kernel(**inputs):
    import numpy as _np
    import concourse.bacc as _bacc
    from concourse import mybir as _mybir
    from concourse.bass_utils import run_bass_kernel_spmd as _run

    nc = _bacc.Bacc("TRN2", target_bir_lowering=False, num_devices=1)
    arrays, args = {}, []
    for name in _INS:
        a = _np.ascontiguousarray(inputs[name])
        arrays[f"in_{name}"] = a
        args.append(nc.dram_tensor(f"in_{name}", a.shape, _mybir.dt.from_np(a.dtype), kind="ExternalInput").ap())
    out = nc.dram_tensor("out_0", (B, T, C), _mybir.dt.float32, kind="ExternalOutput").ap()
    build(nc, *args, out)
    r = _run(nc, [arrays], core_ids=[0])
    return r.results[0]["out_0"]
```

```python
import numpy as np
import concourse.bass as bass
from concourse import mybir
from contextlib import ExitStack

fp32 = mybir.dt.float32
bf16 = mybir.dt.bfloat16
i32 = mybir.dt.int32
u32 = mybir.dt.uint32
u16 = mybir.dt.uint16
ALU = mybir.AluOpType
ACT = mybir.ActivationFunctionType
AX = mybir.AxisListType

P = 128
B, T, C = 4, 1024, 128
H, HD = 16, 8
N = B * T
NT = N // P
BT = T // P
HG = 4
NHG = H // HG
G = B * NHG
HALF = T // 2
QT = HALF // P
PARTS = 3
SPLIT = PARTS * PARTS * HD
ROW_ONE = SPLIT
ROW_ZERO = ROW_ONE + PARTS
ROW_MAX = 99
ROWS = ROW_MAX + PARTS
STEP = 5
STEPS = (P - 1) // STEP
ROWS_DIAG = ROWS + STEPS
E, TOPK, HID = 8, 2, 512
HC = HID // P
SLOT_TILES = N * TOPK // P + E - 1
ROW = C + 2
PAD = 8
PAD_LOADS = -(-SLOT_TILES // PAD)
NEG = -3.0e38
EPS = 1e-5
DEPTH_SCALE = 1.0 / np.sqrt(12)

UNITS = 12
TURN_BANKS = (4, 5, 7)
FIRST_TURNS = UNITS * HG + 1
SEQ = UNITS * HG + 4
LATE_MAX_TURN = 1
RESULT1_TURN = 3 * HG + 1
EARLY_MAX_TURN = 5 * HG + 2
RESULT0_TURN = 7 * HG + 3


class Count:

    def __init__(self, c, i=None, a=0):
        self.c, self.i, self.a = c, i, a

    def __add__(self, k):
        return Count(self.c + k, self.i, self.a)

    def __mul__(self, k):
        return Count(self.c * k, self.i, self.a * k)

    def __floordiv__(self, k):
        assert self.a % k == 0
        return Count(self.c // k, self.i, self.a // k)

    def __mod__(self, k):
        assert self.a % k == 0
        return self.c % k

    def v(self):
        return self.c if self.i is None else self.i * self.a + self.c


def max_unit(u):
    if u < 4:
        return 3 - u, 0, P * (4 - u), True
    if u < 8:
        return u, 0, HALF, False
    return 15 - u, 1, P * (12 - u), True


def prob_unit(u):
    if u < 4:
        return 0, u, P * u, True
    if u < 8:
        return 1, u - 4, 0, False
    return 1, u - 4, P * (u - 8), True


def truncated_parts(a):
    parts, rest = [], a.astype(np.float32)
    for _ in range(PARTS):
        bits = rest.view(np.uint32) & np.uint32(0xFFFF0000)
        parts.append((bits >> 16).astype(np.uint16))
        rest = rest - bits.view(np.float32)
    return parts


def constants(nc):
    start = 2.0 ** (-2.0 ** -(np.log2(H) - 3))
    slopes = np.array([start * start ** i for i in range(H)], np.float32)
    bias = -slopes[:, None] * (T - 1 - np.arange(T, dtype=np.float32))[None, :]
    parts = np.stack(truncated_parts(bias), 1)
    parts = parts.reshape(NHG, HG, PARTS, T).transpose(0, 2, 1, 3)
    alibi = np.tile(parts, (B, 1, 1, 1))
    i = np.arange(P)
    causal = np.zeros((P, HALF), np.float32)
    causal[:, HALF - P:] = np.where(i[None, :] <= i[:, None], 0.0, NEG)
    edge = STEP * (1 + np.arange(STEPS))[:, None]
    fixed_q, fixed_k = np.zeros((2, ROWS_DIAG - ROW_ONE, P), np.uint16)
    one, huge = 0x3F80, 0xF149
    fixed_q[:PARTS] = one
    fixed_q[ROWS - ROW_ONE:] = np.where(i[None, :] < edge, one, 0)
    fixed_k[ROW_MAX - ROW_ONE:ROWS - ROW_ONE] = one
    fixed_k[ROWS - ROW_ONE:] = np.where(i[None, :] >= edge, huge, 0)
    before = np.where(i[:, None] < i[None, :], 0x3F80, 0).astype(np.uint16)
    return (nc.inline_tensor(np.ascontiguousarray(alibi), name="alibi_parts"),
            nc.inline_tensor(np.eye(P, dtype=np.float32), name="identity"),
            nc.inline_tensor(causal, name="causal_bias"),
            nc.inline_tensor(before, name="before_in_tile"),
            nc.inline_tensor(fixed_q, name="fixed_q"), nc.inline_tensor(fixed_k, name="fixed_k"))


def build(nc, x, Wq, bq, Wk, bk, Wv, bv, Wo, bo, Wr, Wg, Wu, Wd, out):
    alibi, eye, causal, before, fixed_q, fixed_k = [t.ap() for t in constants(nc)]
    q_split = nc.dram_tensor("q_split", [G, HG, (2 * PARTS - 1) * HD, T], bf16).ap()
    k_split = nc.dram_tensor("k_split", [G, HG, PARTS * HD, T], bf16).ap()
    slots = nc.dram_tensor("slots", [PAD_LOADS * PAD * P, ROW], fp32).ap()
    routed = nc.dram_tensor("routed", [N * TOPK + PAD * P, C], fp32).ap()

    ctx = ExitStack()
    with ctx:
        def sb(name, shape, dt=fp32):
            return ctx.enter_context(nc.sbuf_tensor(name, shape, dt))

        def sem(name):
            return ctx.enter_context(nc.semaphore(name))

        def sems(name, n=2):
            return [sem(f"{name}{i}") for i in range(n)]

        ps = ctx.enter_context(nc.psum_tensor("ps", [P, 8, HALF], fp32))

        xn = sb("xn", [P, NT * C])
        vall = sb("vall", [P, G * BT * HG * HD])
        attn = sb("attn", [P, G * BT * HG * HD])
        weights = sb("weights", [P, E * 3 * HID])
        wg_sb = weights[:, 0:E * HID]
        wu_sb = weights[:, E * HID:2 * E * HID]
        wd_sb = weights[:, 2 * E * HID:3 * E * HID]
        xb = [weights[:, 0:T], weights[:, T:2 * T]]
        sq = weights[:, 2 * T:3 * T]
        xt = [weights[:, 3 * T:4 * T], weights[:, 4 * T:5 * T]]
        full = [weights[:, 5 * T:6 * T], weights[:, 6 * T:7 * T]]
        rest = [weights[:, 7 * T:8 * T], weights[:, 8 * T:9 * T]]
        prob_sb = sb("prob_sb", [P, 2 * HG * HALF])
        prob = [prob_sb[:, i * HG * HALF:(i + 1) * HG * HALF].rearrange("p (c t) -> p c t", c=HG) for i in range(2)]
        split = [a.bitcast(bf16).rearrange("p (s i t) -> p s i t", s=2, i=PARTS)
                 for a in (weights[:, 9 * T:12 * T], prob_sb[:, 0:3 * T])]
        qs = [sb(f"qs{i}", [ROWS_DIAG, 2, HG, HALF], bf16) for i in range(2)]
        ks = [sb(f"ks{i}", [ROWS_DIAG, 2, HG, HALF], bf16) for i in range(2)]
        vs = [sb(f"vs{i}", [P, BT, HG, 32]) for i in range(2)]
        ot = [sb(f"ot{i}", [P, HALF]) for i in range(2)]
        causal_sb = sb("causal_sb", [P, HALF])
        junk = {i: sb(f"junk{i}", [P, HALF], bf16) for i in TURN_BANKS}
        ident = sb("ident", [P, P])
        before_sb = sb("before_sb", [P, P], bf16)
        ones_bf = sb("ones_bf", [P, P], bf16)
        wq_sb, wk_sb, wv_sb, wo_sb = [sb(n, [P, C]) for n in ("wq_sb", "wk_sb", "wv_sb", "wo_sb")]
        wr_sb = sb("wr_sb", [P, E])
        bias_qk = sb("bias_qk", [P, 2])
        bias_q_scaled = sb("bias_q_scaled", [P, 1])
        bv_row = sb("bv_row", [P, C])
        bo_row = sb("bo_row", [P, C])
        stat = sb("stat", [P, 5, BT])
        mx = sb("mx", [P, 2, HG * QT])
        mx_late = sb("mx_late", [P, HG * QT])
        mx_all = sb("mx_all", [P, HG * QT])
        mt = [sb(f"mt{i}", [HG * QT, PARTS, P], bf16) for i in range(2)]
        negated = [sb(f"negated{i}", [HG * QT, P]) for i in range(2)]
        mrest = [sb(f"mrest{i}", [HG * QT, P]) for i in range(2)]
        rden = sb("rden", [P, 2, HG * QT])
        logits = sb("logits", [P, NT * E])
        rt = [sb(f"rt{i}", [P, NT * E]) for i in range(6)]
        mask_bf = sb("mask_bf", [P, NT * E], bf16)
        rs = sb("rs", [P, 5, NT])
        ex = sb("ex", [P, 6, E])
        exi = sb("exi", [P, 2, E], i32)
        eidx = sb("eidx", [P, NT * E])
        meta = sb("meta", [P, NT, TOPK, 3])
        tile_no = sb("tile_no", [1, SLOT_TILES])
        owner = sb("owner", [1, SLOT_TILES * E])
        owner_f = sb("owner_f", [1, SLOT_TILES])
        owner_i = sb("owner_i", [1, SLOT_TILES], i32)
        stage = [sb(f"stage{i}", [P, ROW]) for i in range(2)]
        stage_idx = [sb(f"stage_idx{i}", [P, 1], u32) for i in range(2)]
        padrow = sb("padrow", [P, PAD, ROW])
        row_in = [sb(f"row_in{i}", [P, ROW]) for i in range(4)]
        row_t = [sb(f"row_t{i}", [P, P]) for i in range(2)]
        gate = [sb(f"gate{i}", [P, HID]) for i in range(2)]
        hid = [sb(f"hid{i}", [P, HID]) for i in range(2)]
        wgu = [sb(f"wgu{i}", [P, 2 * HID]) for i in range(2)]
        y_out = [sb(f"y_out{i}", [P, C]) for i in range(2)]
        y_idx = [sb(f"y_idx{i}", [P, 1], u32) for i in range(4)]
        heads = ot
        xres = vall
        at_sb = [prob_sb[:, i * HALF:(i + 1) * HALF] for i in range(2)]
        yres = [prob_sb[:, i * 2 * HALF:(i + 1) * 2 * HALF] for i in range(2)]
        fin = [prob_sb[:, (4 + i) * HALF:(5 + i) * HALF] for i in range(2)]

        s_const, s_bias, s_fixed, s_ones, s_pad, s_padded, s_iota = [sem("s_" + n) for n in (
            "const", "bias", "fixed", "ones", "pad", "padded", "iota")]
        s_x, s_rest, s_part2, s_part3, s_split = [sems("s_" + n) for n in ("x", "rest", "part2", "part3", "split")]
        s_xc, s_sq, s_var, s_std, s_ln, s_xn, s_xt_ps, s_xt, s_qk_ps, s_qk, s_v_ps, s_v, s_lg_ps, s_lg = [
            sem("s_" + n) for n in ("xc", "sq", "var", "std", "ln", "xn", "xt_ps", "xt", "qk_ps", "qk", "v_ps", "v",
                                    "lg_ps", "lg")]
        s_gap, s_gap_exp, s_mask, s_count, s_meta, s_owner, s_weights = [sem("s_" + n) for n in (
            "gap", "gap_exp", "mask", "count", "meta", "owner", "weights")]
        s_load = [sems(f"s_load{i}_") for i in range(2)]
        s_chunk = sem("s_chunk")
        s_read = sem("s_read")
        s_mx = sem("s_mx")
        s_mpart, s_mrest = sem("s_mpart"), sem("s_mrest")
        s_mt = sem("s_mt")
        s_mrow = sems("s_mrow")
        s_score = sem("s_score")
        s_exp = sem("s_exp")
        s_causal = sem("s_causal")
        s_vcopy = sem("s_vcopy")
        s_pv = sem("s_pv")
        s_ocopy = sem("s_ocopy")
        s_rden = sem("s_rden")
        s_staged = sem("s_staged")
        s_scatter = sems("s_scatter")
        s_xres, s_xbo, s_heads, s_at_ps, s_at, s_wo, s_res = [sem("s_" + n) for n in (
            "xres", "xbo", "heads", "at_ps", "at", "wo", "res")]
        s_row = sems("s_row", 4)
        s_row_ps, s_row_t, s_wgu, s_gate_ps, s_up_ps, s_gate, s_hid, s_y_ps, s_y, s_yidx = [
            sem("s_" + n) for n in ("row_ps", "row_t", "wgu", "gate_ps", "up_ps", "gate", "hid", "y_ps", "y", "yidx")]
        s_routed = sems("s_routed")
        s_yres = sems("s_yres")
        s_acc, s_fin = sem("s_acc"), sem("s_fin")
        s_out = sems("s_out")

        block = ctx.enter_context(nc.Block())
        CONST = 12 * 16
        GROUP_LOAD = 7 * 16

        def wait_apart(eng, waited, count):
            eng.wait_ge(waited, count.v())
            if count.i is not None:
                eng.nop(nofuse=True)

        def loop_of_groups(eng, step, last):
            with eng.Fori(0, last // 2) as i:
                for k in range(2):
                    step(Count(1 + k, i, 2))

        def loop_of_slots(eng, step):
            loops = (SLOT_TILES - 6) // 4
            for s in range(4):
                step(Count(s))
            with eng.Fori(0, loops) as i:
                for k in range(4):
                    step(Count(4 + k, i, 4))
            for s in range(4 + 4 * loops, SLOT_TILES):
                step(Count(s))

        class Turn:

            def __init__(self, number, bank, since):
                self.number, self.bank, self.since = number, TURN_BANKS[bank % 3], since

            def filled(self):
                return self.number + 1

            def read(self):
                return self.number + 1

            def bank_read(self):
                return self.number + (1 - self.since)

        def first_turn(u, h):
            k = HG * u + h
            return first_turn_at(k + (u >= 5))

        def first_turn_at(place):
            return Turn(Count(place), place - FIRST_TURNS, 3 if place >= 3 else None)

        def step_turn(g, place):
            early = not g.a and g.c == 0 and place < RESULT1_TURN
            return Turn(g * SEQ + (FIRST_TURNS - 1 + place + early), max(place - 1, 0),
                        1 if place == 1 else 4 if place in (2, 3) else
                        2 if not g.a and g.c == 0 and RESULT1_TURN < place < RESULT1_TURN + 3 else 3)

        def chunk_turn(g, u, h):
            k = HG * u + h
            return step_turn(g, k + (k >= 1) + (u >= 3) + (u >= 5) + (u >= 7))

        @block.sync
        def _(sp):
            for b in range(2):
                sp.dma_start(xb[b].rearrange("p (j c) -> p j c", c=C),
                             x[b].rearrange("(j p) c -> p j c", p=P)).then_inc(s_x[b], 16)
            for dst, src in ((ident[:, :], eye), (wq_sb[:, :], Wq), (wk_sb[:, :], Wk), (wv_sb[:, :], Wv),
                             (wo_sb[:, :], Wo), (wr_sb[:, :], Wr), (before_sb[:, :].bitcast(u16), before),
                             (causal_sb[:, :], causal),
                             (bias_qk[:, 0:1], bq.rearrange("(c a) -> c a", a=1)),
                             (bias_qk[:, 1:2], bk.rearrange("(c a) -> c a", a=1)),
                             (bv_row[:, :], bv.rearrange("(a c) -> a c", a=1).to_broadcast([P, C])),
                             (bo_row[:, :], bo.rearrange("(a c) -> a c", a=1).to_broadcast([P, C]))):
                sp.dma_start(dst, src).then_inc(s_const, 16)

            def next_tokens(b):
                sp.wait_ge(s_xc, b - 1)
                sp.dma_start(xb[b % 2].rearrange("p (j c) -> p j c", c=C),
                             x[b].rearrange("(j p) c -> p j c", p=P)).then_inc(s_x[b % 2], 16)

            for stacks, fixed in ((qs, fixed_q), (ks, fixed_k)):
                for par in range(2):
                    sp.dma_start(stacks[par][ROW_ONE:ROWS_DIAG, :, :, :].rearrange("r f h t -> r (f h t)")
                                 .rearrange("r (m t) -> r m t", t=P).bitcast(u16),
                                 fixed.unsqueeze(1).to_broadcast([ROWS_DIAG - ROW_ONE, 2 * HG * QT, P])
                                 ).then_inc(s_fixed, 16)

            def load(g, hf):
                par = g % 2
                gi = g.v()
                lo = hf * HALF
                done = s_load[par][hf]
                for i in range(PARTS):
                    rows = slice(i * PARTS * HD, (i + 1) * PARTS * HD)
                    sp.dma_start(qs[par][rows, hf, :, :],
                                 q_split[bass.ds(gi, 1), :, i * HD:(i + PARTS) * HD, lo:lo + HALF]
                                 .rearrange("g h r t -> r (g h) t")).then_inc(done, 16)
                    sp.dma_start(ks[par][rows, hf, :, :],
                                 k_split[bass.ds(gi, 1), :, :, lo:lo + HALF]
                                 .rearrange("g h r t -> r (g h) t")).then_inc(done, 16)
                sp.dma_start(ks[par][ROW_ONE:ROW_ZERO, hf, :, :].bitcast(u16),
                             alibi[bass.ds(gi, 1), :, :, lo:lo + HALF]
                             .rearrange("g i h t -> i (g h) t")).then_inc(done, 16)

            for b in range(B):
                if b + 2 < B:
                    next_tokens(b + 2)
                for s, dst in enumerate((q_split, k_split)):
                    sp.wait_ge(s_part3[s], b + 1)
                    mine = dst[b * NHG:(b + 1) * NHG].rearrange("g h r t -> (g h) r t")
                    for k in range(2 * PARTS - 1 if s == 0 else PARTS):
                        sp.dma_start(mine[:, k * HD:(k + 1) * HD, :],
                                     split[b % 2][:, s, k % PARTS, :]).then_inc(s_split[b % 2], 16)
                if b == 1:
                    sp.wait_ge(s_split[0], 8 * 16)
                    sp.wait_ge(s_fixed, 4 * 16)
                    for g in range(2):
                        for hf in range(2):
                            load(Count(g), hf)
            for i in range(2):
                sp.wait_ge(s_split[i], 8 * 16 * (B // 2))

            def place_maxima(g, hf):
                event = g * 2 + hf
                for i in range(PARTS):
                    sp.wait_ge(*((s_mpart, (event * 2 + (i + 1)).v()) if i < 2 else (s_mt, (event + 1).v())))
                    dst = qs[g % 2][ROW_MAX + i:ROW_MAX + i + 1, hf, :, :].rearrange("p h t -> p (h t)")
                    sp.dma_start(dst.rearrange("p (m t) -> p m t", t=P), mt[hf][:, i, :]).then_inc(s_mrow[hf], 16)

            place_maxima(Count(0), 0)

            def expert_weights(g):
                e = (g + -1).v()
                at = e * HID
                sp.dma_start(wg_sb[:, bass.ds(at, HID)],
                             Wg[bass.ds(e, 1)].rearrange("e c h -> c (e h)")).then_inc(s_weights, 16)
                sp.dma_start(wu_sb[:, bass.ds(at, HID)],
                             Wu[bass.ds(e, 1)].rearrange("e c h -> c (e h)")).then_inc(s_weights, 16)
                sp.dma_start(wd_sb[:, bass.ds(at, HID)].rearrange("p (j c) -> p j c", c=C),
                             Wd[bass.ds(e, 1)].rearrange("e (j p) c -> p (e j) c", p=P)).then_inc(s_weights, 16)

            def step(g, loads=True, maxima=True, weights=False):
                place_maxima(g, 1)
                if maxima:
                    place_maxima(g + 1, 0)
                if weights:
                    expert_weights(g)
                if loads:
                    sp.wait_ge(s_score, (g * 24 + 16).v())
                    load(g + 2, 0)
                    sp.wait_ge(s_score, (g * 24 + 24).v())
                    load(g + 2, 1)

            step(Count(0))
            sp.wait_ge(s_v_ps, B)
            with sp.Fori(0, E // 2) as i:
                for k in range(2):
                    step(Count(1 + k, i, 2), weights=True)
            with sp.Fori(E // 2, (G - 4) // 2) as i:
                for k in range(2):
                    step(Count(1 + k, i, 2))
            step(Count(G - 3))
            step(Count(G - 2), loads=False)
            step(Count(G - 1), loads=False, maxima=False)

            sp.wait_ge(s_vcopy, G)
            for b in range(B):
                sp.dma_start(xres[:, b * T:(b + 1) * T].rearrange("p (j c) -> p j c", c=C),
                             x[b].rearrange("(j p) c -> p j c", p=P)).then_inc(s_xres, 16)

            sp.wait_ge(s_padded, 16 * PAD_LOADS)
            for r in range(TOPK):
                sp.wait_ge(s_scatter[r], 16 * NT)

            def rows(s):
                if s.a or s.c >= 4:
                    sp.wait_ge(s_y, (s + -3).v())
                    sp.wait_ge(s_yidx, (s + -3).v())
                at = s.v() * P if s.a == 0 else s.i * (s.a * P) + s.c * P
                sp.dma_start(row_in[s % 4][:, :], slots[bass.ds(at, P), :]).then_inc(s_row[s % 4], 16)

            for s in range(4):
                rows(Count(s))
            with sp.Fori(1, SLOT_TILES // 4) as i:
                for k in range(4):
                    rows(Count(k, i, 4))
            for s in range(SLOT_TILES // 4 * 4, SLOT_TILES):
                rows(Count(s))

            for r in range(TOPK):
                sp.wait_ge(s_routed[r], 16 * ((SLOT_TILES + 1 - r) // 2))
            for n in range(NT // QT):
                if n >= 2:
                    sp.wait_ge(s_fin, n - 1)
                sp.dma_start(yres[n % 2].rearrange("p (j c) -> p j c", c=TOPK * C),
                             routed[n * QT * P * TOPK:(n + 1) * QT * P * TOPK, :]
                             .rearrange("(j p r) c -> p j (r c)", p=P, r=TOPK)).then_inc(s_yres[n % 2], 16)

        @block.gpsimd
        def _(pool):
            nc.gpsimd.memset(padrow[:, :, :], 0.0).then_inc(s_pad, 1)
            pool.wait_ge(s_pad, 1)
            nc.gpsimd.iota(padrow[:, :, C + 1], pattern=[[P, PAD]], base=N * TOPK, channel_multiplier=1,
                           allow_small_or_imprecise_dtypes=True).then_inc(s_pad, 1)
            nc.gpsimd.memset(ones_bf[:, :], 1.0).then_inc(s_ones, 1)
            for i in range(2):
                nc.gpsimd.memset(vs[i][:, :, :, :], 0.0).then_inc(s_ones, 1)
            pool.wait_ge(s_ones, 3)
            for i in range(2):
                nc.gpsimd.memset(vs[i][:, :, :, HD:HD + 1], 1.0).then_inc(s_ones, 1)
            nc.gpsimd.iota(eidx[:, :], pattern=[[0, NT], [1, E]], base=0, channel_multiplier=0,
                           allow_small_or_imprecise_dtypes=True).then_inc(s_iota, 1)
            nc.gpsimd.iota(tile_no[:, :], pattern=[[1, SLOT_TILES]], base=0, channel_multiplier=0,
                           allow_small_or_imprecise_dtypes=True).then_inc(s_iota, 1)
            nc.gpsimd.iota(meta[:, :, :, 1], pattern=[[TOPK * P, NT], [1, TOPK]], base=0, channel_multiplier=TOPK,
                           allow_small_or_imprecise_dtypes=True).then_inc(s_iota, 1)
            for b in range(B):
                parts = split[b % 2][:, 1]
                pool.wait_ge(s_qk, 4 * b + 4)
                if b:
                    pool.wait_ge(s_part3[1], b)
                nc.gpsimd.tensor_tensor(rest[1], full[1], parts[:, 0, :], ALU.subtract).then_inc(s_rest[1], 1)
                pool.wait_ge(s_rest[1], b + 1)
                nc.gpsimd.tensor_copy(parts[:, 1, :], rest[1]).then_inc(s_part2[1], 1)
                pool.wait_ge(s_part2[1], b + 1)
                nc.gpsimd.tensor_tensor(parts[:, 2, :], rest[1], parts[:, 1, :], ALU.subtract).then_inc(s_part3[1], 1)

            def copy_values(g):
                gi = g.v()
                at = gi * (BT * HG * HD)
                nc.gpsimd.tensor_copy(vs[g % 2][:, :, :, 0:HD].rearrange("p j c d -> p (j c) d"),
                                      vall[:, bass.ds(at, BT * HG * HD)].rearrange("p (m d) -> p m d", d=HD)
                                      ).then_inc(s_vcopy, 1)

            pool.wait_ge(s_v, 2 * B)
            copy_values(Count(0))
            pool.wait_ge(s_meta, 1)
            pool.wait_ge(s_padded, 16 * PAD_LOADS)

            def scatter(g, k, r):
                n = g * 2 + k
                gi = g.v()
                if g.a or n.c >= 1:
                    wait_apart(pool, s_scatter[r], n * 16)
                nc.gpsimd.tensor_copy(stage[r][:, 0:C], xn[:, bass.ds(gi * (2 * C) + k * C, C)]).then_inc(s_staged, 1)
                mine = meta[:, bass.ds(gi * 2 + k, 1), r, :].rearrange("p a m -> p (a m)")
                nc.gpsimd.tensor_copy(stage[r][:, C:ROW], mine[:, 0:2]).then_inc(s_staged, 1)
                nc.gpsimd.tensor_copy(stage_idx[r][:, :], mine[:, 2:3]).then_inc(s_staged, 1)
                wait_apart(pool, s_staged, n * 6 + (3 * r + 3))
                pool.indirect_dma_start(slots[:, :], bass.IndirectOffsetOnAxis(ap=stage_idx[r][:, :], axis=0),
                                        stage[r][:, :], None).then_inc(s_scatter[r], 16)

            def step(g, values=True):
                diagonal = 0
                for u in range(UNITS):
                    if prob_unit(u)[3]:
                        diagonal += 1
                        wait_apart(pool, s_exp, g * 24 + (2 * u + 2))
                        first = prob[u % 2][:, :, 0:P]
                        nc.gpsimd.affine_select(out=first, in_=first, compare_op=ALU.is_ge, fill=0.0, base=0,
                                                pattern=[[0, HG], [1, P]], channel_multiplier=-1).then_inc(s_causal, 1)
                    if u == 3 and values:
                        if g.a or g.c:
                            wait_apart(pool, s_pv, g * UNITS)
                        copy_values(g + 1)
                    if u == 4:
                        for k in range(2):
                            for r in range(TOPK):
                                scatter(g, k, r)

            step(Count(0))
            loop_of_groups(pool, step, G - 2)
            step(Count(G - 1), values=False)

            def put(s):
                pool.wait_ge(s_yidx, (s + 1).v())
                wait_apart(pool, s_y, s + 1)
                pool.indirect_dma_start(routed[:, :], bass.IndirectOffsetOnAxis(ap=y_idx[s % 4][:, :], axis=0),
                                        y_out[s % 2][:, :], None).then_inc(s_routed[s % 2], 16)

            loop_of_slots(pool, put)

        @block.scalar
        def _(act):
            def norm(b):
                act.wait_ge(s_xc, b + 1)
                if b:
                    act.wait_ge(s_var, b)
                nc.scalar.activation(sq, xn[:, b * T:(b + 1) * T], ACT.Square).then_inc(s_sq, 1)
                act.wait_ge(s_var, b + 1)
                if b:
                    act.wait_ge(s_xn, b)
                nc.scalar.activation(stat[:, 2, :], stat[:, 1, :], ACT.Sqrt).then_inc(s_std, 1)

            norm(0)
            act.wait_ge(s_const, CONST)
            nc.scalar.mul(bias_q_scaled[:, :], bias_qk[:, 0:1], HD ** -0.5).then_inc(s_bias, 1)
            act.wait_ge(s_bias, 1)
            for b in range(B):
                for i in range(2):
                    act.wait_ge(s_xt_ps, 2 * b + i + 1)
                    if b >= 2 and i == 0:
                        act.wait_ge(s_v_ps, b - 1)
                    nc.scalar.copy(xt[b % 2][:, i * HALF:(i + 1) * HALF], ps[:, i, :]).then_inc(s_xt, 1)
                if b + 1 < B:
                    norm(b + 1)
                for s in range(2):
                    act.wait_ge(s_qk_ps, 2 * b + s + 1)
                    if b:
                        act.wait_ge(s_part2[s], b)
                    if b >= 2:
                        act.wait_ge(s_split[b % 2], 8 * 16 * (b // 2))
                    src = ps[:, 2 + 2 * s:4 + 2 * s, :].rearrange("p a t -> p (a t)")
                    bias, scale = (bias_q_scaled[:, :], HD ** -0.5) if s == 0 else (bias_qk[:, 1:2], 1.0)
                    for dst in (full[s], split[b % 2][:, s, 0, :]):
                        nc.scalar.activation(dst, src, ACT.Identity, bias=bias, scale=scale).then_inc(s_qk, 1)

            act.wait_ge(s_gap, 1)
            nc.scalar.activation(rs[:, 4, :], rs[:, 3, :], ACT.Exp).then_inc(s_gap_exp, 1)
            act.wait_ge(s_split[1], 8 * 16 * (B // 2))
            act.wait_ge(s_pad, 2)
            for i in range(PAD_LOADS):
                act.dma_start(slots[i * PAD * P:(i + 1) * PAD * P, :].rearrange("(j p) c -> p j c", p=P),
                             padrow[:, :, :]).then_inc(s_padded, 16)


            def take_out(g, hf):
                act.wait_ge(s_pv, (g * UNITS + (4 if hf == 0 else UNITS)).v())
                nc.scalar.copy(ot[hf][:, :], ps[:, 6, :]).then_inc(s_ocopy, 1)

            def step(g):
                for u in range(UNITS):
                    q0 = prob_unit(u)[2]
                    n = HALF - q0
                    if g.a or g.c or u >= 2:
                        act.wait_ge(s_pv, (g * UNITS + (u - 1)).v())
                    for pair in range(2):
                        act.wait_ge(s_score, (g * 24 + (2 * u + pair + 1)).v())
                        nc.scalar.activation(prob[u % 2][:, 2 * pair:2 * pair + 2, 0:n],
                                             ps[:, 2 * pair:2 * pair + 2, 0:n], ACT.Exp).then_inc(s_exp, 1)
                    if u == 0 and (g.a or g.c):
                        take_out(g + -1, 1)
                    if u == 4:
                        take_out(g, 0)

            step(Count(0))
            loop_of_groups(act, step, G - 2)
            step(Count(G - 1))
            take_out(Count(G - 1), 1)

            def copy_row(s):
                act.wait_ge(s_row_ps, (s + 1).v())
                nc.scalar.copy(row_t[s % 2][:, :], ps[:, 4 + s % 2, 0:P]).then_inc(s_row_t, 1)

            act.wait_ge(s_pv, UNITS * G)
            for n in range(NT // QT):
                act.wait_ge(s_at_ps, n + 1)
                if n >= 2:
                    act.wait_ge(s_wo, n - 1)
                nc.scalar.copy(at_sb[n % 2][:, :], ps[:, n % 2, :]).then_inc(s_at, 1)
                if n == 0:
                    copy_row(Count(0))
                    copy_row(Count(1))

            def silu(s):
                act.wait_ge(s_gate_ps, (s + 1).v())
                if s.a or s.c >= 2:
                    act.wait_ge(s_hid, (s + -1).v())
                nc.scalar.activation(gate[s % 2][:, :], ps[:, s % 2, :], ACT.Silu).then_inc(s_gate, 1)

            def weigh(s):
                act.wait_ge(s_y_ps, (s + 1).v())
                if s.a or s.c >= 2:
                    act.wait_ge(s_routed[s % 2], (s // 2 * 16).v())
                nc.scalar.activation(y_out[s % 2][:, :], ps[:, 6 + s % 2, 0:C], ACT.Copy,
                                     scale=row_in[s % 4][:, C:C + 1]).then_inc(s_y, 1)

            act.wait_ge(s_res, NT // QT)
            silu(Count(0))

            def expert(s):
                peeled = not s.a
                if not peeled or s.c + 1 < SLOT_TILES:
                    silu(s + 1)
                if not peeled or s.c + 2 < SLOT_TILES:
                    copy_row(s + 2)
                weigh(s)

            loop_of_slots(act, expert)
            for n in range(NT // QT):
                act.wait_ge(s_fin, n + 1)
                b, hf = divmod(n, 2)
                act.dma_start(out[b, hf * HALF:(hf + 1) * HALF].rearrange("(j p) c -> p j c", p=P),
                              fin[n % 2].rearrange("p (j c) -> p j c", c=C)).then_inc(s_out[n % 2], 16)
            for i in range(2):
                act.wait_ge(s_out[i], 16 * (NT // QT // 2))

        @block.vector
        def _(dve):
            chain = [0]

            def link(ins):
                chain[0] += 1
                ins.then_inc(s_ln, 1)
                dve.wait_ge(s_ln, chain[0])

            inv, var, std, r, t = [stat[:, i, :] for i in range(5)]

            def col(a):
                return a.unsqueeze(2).to_broadcast([P, BT, C])

            def tiles(a):
                return a.rearrange("p (j c) -> p j c", c=C)

            def norm(b):
                dve.wait_ge(s_x[b % 2], 16 * (b // 2 + 1))
                link(nc.vector.tensor_reduce(inv, tiles(xb[b % 2]), AX.X, ALU.add))
                link(nc.vector.tensor_scalar(t, inv, 1.0 / C, None, ALU.mult))
                mine = tiles(xn[:, b * T:(b + 1) * T])
                nc.vector.tensor_tensor(mine, tiles(xb[b % 2]), col(t), ALU.subtract).then_inc(s_xc, 1)
                dve.wait_ge(s_sq, b + 1)
                link(nc.vector.tensor_reduce(inv, tiles(sq), AX.X, ALU.add))
                nc.vector.tensor_scalar(var, inv, 1.0 / C, EPS, ALU.mult, ALU.add).then_inc(s_var, 1)
                dve.wait_ge(s_var, b + 1)
                dve.wait_ge(s_std, b + 1)
                link(nc.vector.reciprocal(r, std))
                link(nc.vector.tensor_tensor(t, r, r, ALU.mult))
                link(nc.vector.tensor_tensor(t, t, var, ALU.mult))
                link(nc.vector.tensor_scalar(t, t, -0.5, 1.5, ALU.mult, ALU.add))
                link(nc.vector.tensor_tensor(t, t, r, ALU.mult))
                nc.vector.tensor_tensor(mine, mine, col(t), ALU.mult).then_inc(s_xn, 1)

            def split_queries(b):
                parts = split[b % 2][:, 0]
                if b:
                    dve.wait_ge(s_part3[0], b)
                dve.wait_ge(s_qk, 4 * b + 2)
                nc.vector.tensor_tensor(rest[0], full[0], parts[:, 0, :], ALU.subtract).then_inc(s_rest[0], 1)
                dve.wait_ge(s_rest[0], b + 1)
                nc.vector.tensor_copy(parts[:, 1, :], rest[0]).then_inc(s_part2[0], 1)
                dve.wait_ge(s_part2[0], b + 1)
                nc.vector.tensor_tensor(parts[:, 2, :], rest[0], parts[:, 1, :], ALU.subtract).then_inc(s_part3[0], 1)

            def values(b):
                dve.wait_ge(s_v_ps, b + 1)
                dst = vall[:, b * T:(b + 1) * T].rearrange("p (g j c) -> p j g c", g=NHG, j=BT)
                for i in range(2):
                    for j in range(4):
                        last = nc.vector.tensor_tensor(
                            dst[:, 4 * i + j],
                            ps[:, 6 + i, j * P:(j + 1) * P].rearrange("p (g c) -> p g c", g=NHG),
                            bv_row[:, :].rearrange("p (g c) -> p g c", g=NHG), ALU.add)
                    last.then_inc(s_v, 1)

            norm(0)
            dve.wait_ge(s_const, CONST)
            for b in range(B):
                if b + 1 < B:
                    norm(b + 1)
                dve.wait_ge(s_lg_ps, b + 1)
                nc.vector.tensor_copy(logits[:, b * BT * E:(b + 1) * BT * E], ps[:, 0, 0:BT * E]).then_inc(s_lg, 1)
                split_queries(b)
                values(b)

            def by_token(a):
                return a.rearrange("p (n e) -> p n e", e=E)

            def over_e(a):
                return a.unsqueeze(2).to_broadcast([P, NT, E])

            hit, pick1, pick2, masked, work, pos = [by_token(a[:, :]) for a in rt]
            lg, ei = by_token(logits[:, :]), by_token(eidx[:, :])
            v1, v2, idx, gap, egap = [rs[:, i, :] for i in range(5)]
            dve.wait_ge(s_lg, B)
            dve.wait_ge(s_iota, 3)

            def top(values, best, pick):
                link(nc.vector.tensor_reduce(best, values, AX.X, ALU.max))
                link(nc.vector.tensor_tensor(hit, values, over_e(best), ALU.is_equal))
                link(nc.vector.scalar_tensor_tensor(work, hit, -float(E), ei, ALU.mult, ALU.add))
                link(nc.vector.tensor_reduce(idx, work, AX.X, ALU.min))
                link(nc.vector.tensor_scalar(idx, idx, float(E), None, ALU.add))
                link(nc.vector.tensor_tensor(pick, ei, over_e(idx), ALU.is_equal))

            top(lg, v1, pick1)
            link(nc.vector.scalar_tensor_tensor(masked, pick1, NEG, lg, ALU.mult, ALU.add))
            top(masked, v2, pick2)
            nc.vector.tensor_tensor(gap, v2, v1, ALU.subtract).then_inc(s_gap, 1)
            nc.vector.tensor_tensor(by_token(mask_bf[:, :]), pick1, pick2, ALU.add).then_inc(s_mask, 1)
            dve.wait_ge(s_gap_exp, 1)
            link(nc.vector.tensor_scalar(v1, egap, 1.0, None, ALU.add))
            link(nc.vector.reciprocal(v2, v1))
            link(nc.vector.tensor_scalar(v2, v2, float(DEPTH_SCALE), None, ALU.mult))
            nc.vector.tensor_copy(meta[:, :, 0, 0], v2)
            link(nc.vector.tensor_tensor(meta[:, :, 1, 0], v2, egap, ALU.mult))
            dve.wait_ge(s_count, 1)
            counts, upto, start = rt[3][:, :], rt[4][:, :], rt[0][:, :]
            ones_row = rt[5][:, :]
            link(nc.vector.memset(ones_row, 1.0))
            link(nc.vector.tensor_copy(counts.rearrange("p (e n) -> p e n", e=E),
                                       ps[:, 1, 0:NT * E].rearrange("p (n e) -> p e n", e=E)))
            link(nc.vector.tensor_tensor_scan(upto, ones_row, counts, 0.0, ALU.mult, ALU.add))
            link(nc.vector.tensor_tensor(start, upto, counts, ALU.subtract))
            by_e = [a.rearrange("p (e n) -> p e n", e=E) for a in (upto, start)]
            link(nc.vector.tensor_tensor(ex[:, 0, :], by_e[0][:, :, NT - 1], by_e[1][:, :, 0], ALU.subtract))
            link(nc.vector.tensor_scalar(exi[:, 0, :], ex[:, 0, :], float(P - 1), None, ALU.add))
            link(nc.vector.tensor_scalar(exi[:, 1, :], exi[:, 0, :], int(np.log2(P)), None, ALU.logical_shift_right))
            link(nc.vector.tensor_copy(ex[:, 1, :], exi[:, 1, :]))
            link(nc.vector.tensor_tensor_scan(ex[:, 2, :], ones_row[:, 0:E], ex[:, 1, :], 0.0, ALU.mult, ALU.add))
            link(nc.vector.tensor_tensor(ex[:, 3, :], ex[:, 2, :], ex[:, 1, :], ALU.subtract))
            link(nc.vector.scalar_tensor_tensor(ex[:, 4, :], ex[:, 3, :], float(P), by_e[1][:, :, 0],
                                                ALU.mult, ALU.subtract))
            link(nc.vector.tensor_tensor(by_token(counts), by_e[1].rearrange("p e n -> p n e"),
                                         by_token(ps[:, 0, 0:NT * E]), ALU.add))
            link(nc.vector.tensor_tensor(pos, by_token(counts),
                                         ex[:, 4, :].unsqueeze(1).to_broadcast([P, NT, E]), ALU.add))
            for k, pick in enumerate((pick1, pick2)):
                link(nc.vector.tensor_tensor(work, pick, pos, ALU.mult))
                last = nc.vector.tensor_reduce(meta[:, :, k, 2], work, AX.X, ALU.add)
                if k == 0:
                    link(last)
            last.then_inc(s_meta, 1)
            own = owner[:, :].rearrange("p (n e) -> p n e", e=E)
            link(nc.vector.tensor_tensor(own, ex[0:1, 2, :].unsqueeze(1).to_broadcast([1, SLOT_TILES, E]),
                                         tile_no[:, :].unsqueeze(2).to_broadcast([1, SLOT_TILES, E]), ALU.is_le))
            link(nc.vector.tensor_reduce(owner_f[:, :], own, AX.X, ALU.add))
            nc.vector.tensor_scalar(owner_i[:, :], owner_f[:, :], float(E - 1), None, ALU.min).then_inc(s_owner, 1)

            def read_chunk(g, turn, u, h):
                qt, kh, n, diagonal = max_unit(u)
                dst = mx_late[:, :] if kh else mx[:, qt // QT, :]
                dst = dst[:, h * QT + qt % QT:h * QT + qt % QT + 1]
                src = ps[:, turn.bank, 0:n]
                if diagonal:
                    wait_apart(dve, s_chunk, turn.filled())
                else:
                    dve.wait_ge(s_chunk, turn.filled().v())
                if diagonal:
                    ins = nc.vector.tensor_tensor_reduce(out=junk[turn.bank][:, 0:n], in0=src, in1=causal_sb[:, HALF - n:HALF],
                                                         scale=1.0, scalar=NEG, op0=ALU.add, op1=ALU.max,
                                                         accum_out=dst)
                else:
                    ins = nc.vector.tensor_reduce(dst, src, AX.X, ALU.max)
                ins.then_inc(s_read, 1)

            def join_maxima(g, turn):
                dve.wait_ge(s_read, turn.read().v())
                nc.vector.tensor_tensor(mx_all[:, :], mx[:, 1, :], mx_late[:, :], ALU.max).then_inc(s_mx, 1)

            def split_maxima(g, hf, turn, stage):
                event = g * 2 + hf
                dst = mt[hf]
                if stage == 0:
                    dve.wait_ge(s_chunk, turn.filled().v())
                    if g.a or g.c:
                        dve.wait_ge(s_mt, (event + -1).v())
                    nc.vector.tensor_scalar(negated[hf][:, :], ps[0:HG * QT, turn.bank, 0:P], -1.0, None,
                                            ALU.mult).then_inc(s_read, 1)
                elif stage == 1:
                    dve.wait_ge(s_read, turn.read().v())
                    if g.a or g.c:
                        dve.wait_ge(s_mrow[hf], (g * (PARTS * 16)).v())
                    nc.vector.tensor_copy(dst[:, 0, :], negated[hf][:, :]).then_inc(s_mpart, 1)
                elif stage == 2:
                    dve.wait_ge(s_mpart, (event * 2 + 1).v())
                    nc.vector.tensor_tensor(mrest[hf][:, :], negated[hf][:, :], dst[:, 0, :],
                                            ALU.subtract).then_inc(s_mrest, 1)
                elif stage == 3:
                    dve.wait_ge(s_mrest, (event + 1).v())
                    nc.vector.tensor_copy(dst[:, 1, :], mrest[hf][:, :]).then_inc(s_mpart, 1)
                else:
                    dve.wait_ge(s_mpart, (event * 2 + 2).v())
                    nc.vector.tensor_tensor(dst[:, 2, :], mrest[hf][:, :], dst[:, 1, :], ALU.subtract
                                            ).then_inc(s_mt, 1)

            def divide(g, hf, turn):
                dve.wait_ge(s_chunk, turn.filled().v())
                src = ps[:, turn.bank, :].rearrange("p (m w) -> p m w", w=32)
                nc.vector.reciprocal(rden[:, hf, :], src[:, :, HD]).then_inc(s_rden, 1)
                dve.wait_ge(s_rden, (g * 2 + (hf + 1)).v())
                at = g.v() * (BT * HG * HD) + hf * P
                nc.vector.tensor_tensor(attn[:, bass.ds(at, P)].rearrange("p (m d) -> p m d", d=HD),
                                        src[:, :, 0:HD],
                                        rden[:, hf, :].unsqueeze(2).to_broadcast([P, HG * QT, HD]),
                                        ALU.mult).then_inc(s_read, 1)

            for u in range(UNITS):
                for h in range(HG):
                    read_chunk(Count(0), first_turn(u, h), u, h)
                if u == 4:
                    for stage in range(5):
                        split_maxima(Count(0), 0, first_turn_at(5 * HG), stage)
            join_maxima(Count(0), first_turn_at(FIRST_TURNS - 1))

            def step(g, ahead=True):
                late_max, result1, result0 = [step_turn(g, place) for place in (
                    (LATE_MAX_TURN, RESULT1_TURN, RESULT0_TURN) if ahead else (0, 1, 2))]
                for u in range(UNITS):
                    for h in range(HG):
                        at = HG * u + h
                        if ahead:
                            read_chunk(g + 1, chunk_turn(g, u, h), u, h)
                        if at <= 4:
                            split_maxima(g, 1, late_max, at)
                        if 4 * HG + 3 <= at <= 5 * HG + 3 and ahead:
                            split_maxima(g + 1, 0, step_turn(g, EARLY_MAX_TURN), at - (4 * HG + 3))
                    if u == 2 and (g.a or g.c):
                        divide(g + -1, 1, result1)
                    if u == 6:
                        divide(g, 0, result0)
                if ahead:
                    join_maxima(g + 1, step_turn(g, SEQ - 1))

            def copy_weights(s):
                if s.a or s.c >= 2:
                    dve.wait_ge(s_up_ps, (s + -1).v())
                e = dve.value_load(owner_i[0:1, bass.ds(s.v(), 1)], min_val=0, max_val=E - 1)
                both = weights[:, 0:2 * E * HID].rearrange("p (w x) -> p w x", w=2)
                nc.vector.tensor_copy(wgu[s % 2].rearrange("p (w x) -> p w x", w=2),
                                      both[:, :, bass.ds(e * HID, HID)]).then_inc(s_wgu, 1)

            step(Count(0))
            loop_of_groups(dve, step, G - 2)
            step(Count(G - 1), ahead=False)
            dve.wait_ge(s_xres, B * 16)
            for b in range(B):
                nc.vector.tensor_tensor(tiles(xres[:, b * T:(b + 1) * T]), tiles(xres[:, b * T:(b + 1) * T]),
                                        bo_row[:, :].unsqueeze(1).to_broadcast([P, BT, C]), ALU.add).then_inc(s_xbo, 1)
            dve.wait_ge(s_weights, 3 * E * 16)
            dve.wait_ge(s_owner, 1)
            copy_weights(Count(0))
            copy_weights(Count(1))
            divide(Count(G - 1), 1, step_turn(Count(G - 1), 3))

            for r in range(TOPK):
                dve.wait_ge(s_scatter[r], 16 * NT)
            dve.wait_ge(s_read, step_turn(Count(G - 1), 3).read().v())
            dve.wait_ge(s_xbo, B)

            def gather_heads(n):
                b, hf = divmod(n, 2)
                if n >= 2:
                    dve.wait_ge(s_at_ps, n - 1)
                src = attn[:, b * T:(b + 1) * T].rearrange("p (g j c) -> p j g c", g=NHG, j=BT)
                dst = heads[n % 2][:, :].rearrange("p (j g c) -> p j g c", j=QT, g=NHG)
                nc.vector.tensor_copy(dst, src[:, hf * QT:(hf + 1) * QT]).then_inc(s_heads, 1)

            gather_heads(0)
            gather_heads(1)
            for n in range(NT // QT):
                if n + 2 < NT // QT:
                    gather_heads(n + 2)
                dve.wait_ge(s_wo, n + 1)
                nc.vector.tensor_tensor(xn[:, n * HALF:(n + 1) * HALF], ps[:, 2 + n % 2, :],
                                        xres[:, n * HALF:(n + 1) * HALF], ALU.add).then_inc(s_res, 1)

            def multiply(s):
                dve.wait_ge(s_gate, (s + 1).v())
                dve.wait_ge(s_up_ps, (s + 1).v())
                if s.a or s.c >= 2:
                    dve.wait_ge(s_y_ps, (s + -1).v())
                nc.vector.tensor_tensor(hid[s % 2][:, :], ps[:, 2 + s % 2, :], gate[s % 2][:, :],
                                        ALU.mult).then_inc(s_hid, 1)

            def expert(s):
                peeled = not s.a
                multiply(s)
                if not peeled or s.c + 2 < SLOT_TILES:
                    copy_weights(s + 2)
                dve.wait_ge(s_row[s % 4], (s // 4 * 16 + 16).v())
                if not peeled or s.c >= 4:
                    dve.wait_ge(s_routed[s % 2], (s // 2 * 16 + -16).v())
                nc.vector.tensor_copy(y_idx[s % 4][:, :], row_in[s % 4][:, C + 1:C + 2]).then_inc(s_yidx, 1)

            loop_of_slots(dve, expert)

            for n in range(NT // QT):
                dve.wait_ge(s_yres[n % 2], 16 * (n // 2 + 1))
                y = yres[n % 2].rearrange("p (j r c) -> p j r c", r=TOPK, c=C)
                mine = tiles(xn[:, n * HALF:(n + 1) * HALF])
                nc.vector.tensor_tensor(mine, mine, y[:, :, 0, :], ALU.add).then_inc(s_acc, 1)
                dve.wait_ge(s_acc, n + 1)
                if n >= 2:
                    dve.wait_ge(s_out[n % 2], 16 * (n // 2))
                nc.vector.tensor_tensor(tiles(fin[n % 2]), mine, y[:, :, 1, :], ALU.add).then_inc(s_fin, 1)

        @block.tensor
        def _(pe):
            pe.wait_ge(s_const, CONST)
            for b in range(B):
                pe.wait_ge(s_xn, b + 1)
                if b:
                    pe.wait_ge(s_xt, 2 * b)
                    pe.wait_ge(s_lg, b)
                for j in range(BT):
                    last = nc.tensor.transpose(ps[:, j // 4, (j % 4) * P:(j % 4 + 1) * P],
                                               xn[:, b * T + j * C:b * T + (j + 1) * C], ident[:, :])
                    if j % 4 == 3:
                        last.then_inc(s_xt_ps, 1)
                pe.wait_ge(s_xt, 2 * b + 2)
                for j in range(BT):
                    last = nc.tensor.matmul(ps[:, 0, j * E:(j + 1) * E], xt[b % 2][:, j * P:(j + 1) * P],
                                            wr_sb[:, :], start=True, stop=True)
                last.then_inc(s_lg_ps, 1)
                for s, w in enumerate((wq_sb, wk_sb)):
                    if b:
                        pe.wait_ge(s_qk, 4 * (b - 1) + 2 * s + 2)
                    for i in range(2):
                        last = nc.tensor.matmul(ps[:, 2 + 2 * s + i, :], w[:, :],
                                                xt[b % 2][:, i * HALF:(i + 1) * HALF], start=True, stop=True)
                    last.then_inc(s_qk_ps, 1)
                if b:
                    pe.wait_ge(s_v, 2 * b)
                for j in range(BT):
                    last = nc.tensor.matmul(ps[:, 6 + j // 4, (j % 4) * P:(j % 4 + 1) * P],
                                            xt[b % 2][:, j * P:(j + 1) * P], wv_sb[:, :], start=True, stop=True)
                last.then_inc(s_v_ps, 1)

            pe.wait_ge(s_mask, 1)
            pe.wait_ge(s_ones, 1)
            nc.tensor.matmul(ps[:, 0, 0:NT * E], before_sb[:, :], mask_bf[:, :], start=True, stop=True)
            nc.tensor.matmul(ps[:, 1, 0:NT * E], ones_bf[:, :], mask_bf[:, :], start=True, stop=True
                             ).then_inc(s_count, 1)

            def chunk(g, turn, u, h):
                qt, kh, n, _ = max_unit(u)
                if turn.since:
                    pe.wait_ge(s_read, turn.bank_read().v())
                nc.tensor.matmul(ps[:, turn.bank, 0:n],
                                 qs[g % 2][0:ROW_MAX, qt // QT, h, (qt % QT) * P:(qt % QT + 1) * P],
                                 ks[g % 2][0:ROW_MAX, kh, h, 0:n], start=True, stop=True).then_inc(s_chunk, 1)

            def wait_stacks(g, u):
                if u in (0, 4):
                    pe.wait_ge(s_load[g % 2][u // 4], (g // 2 * GROUP_LOAD + GROUP_LOAD).v())

            def transpose_maxima(src, turn):
                pe.wait_ge(s_read, turn.bank_read().v())
                nc.tensor.transpose(ps[0:HG * QT, turn.bank, 0:P], src, ident[:, :]).then_inc(s_chunk, 1)

            def scores(g, u, pair):
                hf, kt, q0, diagonal = prob_unit(u)
                if pair == 0 and u in (0, 4):
                    pe.wait_ge(s_mrow[u // 4], (g * (PARTS * 16) + PARTS * 16).v())
                if g.a or g.c or u:
                    pe.wait_ge(s_exp, (g * 24 + (2 * u + pair - 1)).v())
                pieces = [(ROWS_DIAG, q0, q0 + P)] * diagonal + [(ROWS, q0 + P * diagonal, HALF)]
                for h in (2 * pair, 2 * pair + 1):
                    for rows, lo, hi in pieces:
                        if lo < hi:
                            last = nc.tensor.matmul(ps[:, h, lo - q0:hi - q0],
                                                    ks[g % 2][0:rows, kt // QT, h, (kt % QT) * P:(kt % QT + 1) * P],
                                                    qs[g % 2][0:rows, hf, h, lo:hi], start=True, stop=True)
                last.then_inc(s_score, 1)

            def products(g, u, piece):
                hf, kt, q0, diagonal = prob_unit(u)
                lo = q0 + piece * 2 * P
                hi = min(lo + 2 * P, HALF)
                if lo >= HALF:
                    return
                if piece == 0:
                    if diagonal:
                        pe.wait_ge(s_causal, (g * 8 + (u + 1 if u < 4 else u - 3)).v())
                    else:
                        pe.wait_ge(s_exp, (g * 24 + (2 * u + 2)).v())
                    if u == 0:
                        pe.wait_ge(s_vcopy, (g + 1).v())
                    if u == 4 or u == 0 and (g.a or g.c):
                        pe.wait_ge(s_ocopy, (g * 2 + (u == 4)).v())
                for h in range(HG):
                    last = nc.tensor.matmul(ps[32 * h:32 * h + 32, 6, lo:hi], vs[g % 2][:, kt, h, :],
                                            prob[u % 2][:, h, lo - q0:hi - q0],
                                            start=(kt == 0 and piece == 0),
                                            stop=(kt == (QT - 1 if hf == 0 else BT - 1)))
                if hi == HALF:
                    last.then_inc(s_pv, 1)

            def transpose_result(g, hf, turn):
                pe.wait_ge(s_ocopy, (g * 2 + (hf + 1)).v())
                pe.wait_ge(s_read, turn.bank_read().v())
                for j in range(QT):
                    last = nc.tensor.transpose(ps[:, turn.bank, j * P:(j + 1) * P], ot[hf][:, j * P:(j + 1) * P],
                                               ident[:, :])
                last.then_inc(s_chunk, 1)

            pe.wait_ge(s_ones, 5)
            pe.wait_ge(s_fixed, 4 * 16)
            pe.wait_ge(s_qk, 4 * B)
            pe.wait_ge(s_v, 2 * B)
            for u in range(UNITS):
                wait_stacks(Count(0), u)
                for h in range(HG):
                    chunk(Count(0), first_turn(u, h), u, h)
                if u == 4:
                    transpose_maxima(mx[:, 0, :], first_turn_at(5 * HG))
            pe.wait_ge(s_meta, 1)
            for pair in range(2):
                scores(Count(0), 0, pair)

            def step(g, ahead=True):
                late_max, result1, result0 = [step_turn(g, place) for place in (
                    (LATE_MAX_TURN, RESULT1_TURN, RESULT0_TURN) if ahead else (0, 1, 2))]
                for u in range(UNITS):
                    if ahead:
                        wait_stacks(g + 1, u)
                    for pair in range(2):
                        if ahead:
                            chunk(g + 1, chunk_turn(g, u, pair), u, pair)
                        if u + 1 < UNITS:
                            scores(g, u + 1, pair)
                        elif ahead:
                            scores(g + 1, 0, pair)
                        if u == 0 and pair == 0:
                            pe.wait_ge(s_mx, (g + 1).v())
                            transpose_maxima(mx_all[:, :], late_max)
                    for piece in range(2):
                        if ahead:
                            chunk(g + 1, chunk_turn(g, u, 2 + piece), u, 2 + piece)
                        products(g, u, piece)
                    if u == 2 and (g.a or g.c):
                        transpose_result(g + -1, 1, result1)
                    if u == 4 and ahead:
                        pe.wait_ge(s_read, chunk_turn(g, 3, HG - 1).read().v())
                        transpose_maxima(mx[:, 0, :], step_turn(g, EARLY_MAX_TURN))
                    if u == 6:
                        transpose_result(g, 0, result0)

            step(Count(0))
            loop_of_groups(pe, step, G - 2)
            step(Count(G - 1), ahead=False)
            transpose_result(Count(G - 1), 1, step_turn(Count(G - 1), 3))

            def expert_of(s):
                return pe.value_load(owner_i[0:1, bass.ds(s.v(), 1)], min_val=0, max_val=E - 1)

            def transpose_row(s):
                pe.wait_ge(s_row[s % 4], (s // 4 * 16 + 16).v())
                if s.a or s.c >= 2:
                    pe.wait_ge(s_row_t, (s + -1).v())
                nc.tensor.transpose(ps[:, 4 + s % 2, 0:P], row_in[s % 4][:, 0:C], ident[:, :]).then_inc(s_row_ps, 1)

            def transpose_heads(n):
                if n >= 2:
                    pe.wait_ge(s_at, n - 1)
                pe.wait_ge(s_heads, n + 1)
                for j in range(QT):
                    last = nc.tensor.transpose(ps[:, n % 2, j * P:(j + 1) * P], heads[n % 2][:, j * P:(j + 1) * P],
                                               ident[:, :])
                last.then_inc(s_at_ps, 1)

            pe.wait_ge(s_exp, 24 * G)
            transpose_heads(0)
            transpose_row(Count(0))
            transpose_row(Count(1))
            for n in range(NT // QT):
                if n + 1 < NT // QT:
                    transpose_heads(n + 1)
                pe.wait_ge(s_at, n + 1)
                if n >= 2:
                    pe.wait_ge(s_res, n - 1)
                for j in range(QT):
                    last = nc.tensor.matmul(ps[:, 2 + n % 2, j * P:(j + 1) * P],
                                            at_sb[n % 2][:, j * P:(j + 1) * P], wo_sb[:, :], start=True, stop=True)
                last.then_inc(s_wo, 1)

            pe.wait_ge(s_owner, 1)
            pe.wait_ge(s_weights, 3 * E * 16)
            pe.wait_ge(s_res, NT // QT)

            def gate_up(s):
                pe.wait_ge(s_wgu, (s + 1).v())
                pe.wait_ge(s_row_t, (s + 1).v())
                if s.a or s.c >= 2:
                    pe.wait_ge(s_hid, (s + -1).v())
                for w, done in enumerate((s_gate_ps, s_up_ps)):
                    for j in range(HC):
                        at = w * HID + j * P
                        last = nc.tensor.matmul(ps[:, 2 * w + s % 2, j * P:(j + 1) * P], wgu[s % 2][:, at:at + P],
                                                row_t[s % 2][:, :], start=True, stop=True)
                    last.then_inc(done, 1)

            def down(s):
                e = expert_of(s)
                pe.wait_ge(s_hid, (s + 1).v())
                if s.a or s.c >= 2:
                    pe.wait_ge(s_y, (s + -1).v())
                for j in range(HC):
                    last = nc.tensor.matmul(ps[:, 6 + s % 2, 0:C], hid[s % 2][:, j * P:(j + 1) * P],
                                            wd_sb[:, bass.ds(e * HID + j * C, C)], start=(j == 0), stop=(j == HC - 1))
                last.then_inc(s_y_ps, 1)

            gate_up(Count(0))

            def expert(s):
                peeled = not s.a
                if not peeled or s.c + 1 < SLOT_TILES:
                    gate_up(s + 1)
                if not peeled or s.c + 2 < SLOT_TILES:
                    transpose_row(s + 2)
                down(s)

            loop_of_slots(pe, expert)


_INS = ['L0_attn_x', 'L0_attn_Wq', 'L0_attn_bq', 'L0_attn_Wk', 'L0_attn_bk', 'L0_attn_Wv', 'L0_attn_bv',
        'L0_attn_Wo', 'L0_attn_bo', 'L0_ffn_Wr', 'L0_ffn_Wg', 'L0_ffn_Wu', 'L0_ffn_Wd']


def kernel(**inputs):
    import numpy as _np
    import concourse.bacc as _bacc
    from concourse import mybir as _mybir
    from concourse.bass_utils import run_bass_kernel_spmd as _run

    nc = _bacc.Bacc("TRN2", target_bir_lowering=False, num_devices=1)
    arrays, args = {}, []
    for name in _INS:
        a = _np.ascontiguousarray(inputs[name])
        arrays[f"in_{name}"] = a
        args.append(nc.dram_tensor(f"in_{name}", a.shape, _mybir.dt.from_np(a.dtype), kind="ExternalInput").ap())
    out = nc.dram_tensor("out_0", (B, T, C), _mybir.dt.float32, kind="ExternalOutput").ap()
    build(nc, *args, out)
    r = _run(nc, [arrays], core_ids=[0])
    return r.results[0]["out_0"]
```
